# Optimizing a Trainium2 kernel written in Bass

```python
import numpy as np
import jax
import jax.numpy as jnp

def _softmax(x, axis=-1):
    return jax.nn.softmax(x, axis=axis)

def _gelu(x):
    return jax.nn.gelu(x, approximate=True)

def _silu(x):
    return jax.nn.silu(x)

def _sigmoid(x):
    return jax.nn.sigmoid(x)

def _layernorm(x, axis=-1, eps=1e-05):
    m = jnp.mean(x, axis=axis, keepdims=True)
    v = jnp.var(x, axis=axis, keepdims=True)
    return (x - m) / jnp.sqrt(v + eps)

def _scatter_add(tgt, idx, src, axis=0):
    return tgt.at[idx].add(src)

def _segment_sum(src, seg, n):
    return jax.ops.segment_sum(src, seg, n)
kernel_name = 'mk_adaln_ffn_d2_seqx_r4_fd8ebe'

def setup_inputs(seed: int=0):
    np.random.seed(seed)
    _w = jnp.asarray

    def _rec_inputs():
        import jax
        import jax.numpy as jnp
        _rk = jax.random.key(seed)
        x = 0.0001734 + 0.8201 * jax.random.normal(jax.random.fold_in(_rk, 1), (128, 64, 1024), jnp.float32)
        _lenS = 64 - jax.random.randint(jax.random.fold_in(_rk, 7), (128,), 0, max(1, 64 // 4) + 1, jnp.int32)
        _lenS2 = 64 - jax.random.randint(jax.random.fold_in(_rk, 8), (128,), 0, max(1, 64 // 4) + 1, jnp.int32)
        itok_B_0_7 = jax.random.randint(jax.random.fold_in(_rk, 11), (128,), 0, 8, jnp.int32)
        itok_B_2182_4065 = jax.random.randint(jax.random.fold_in(_rk, 13), (128,), 2182, 4066, jnp.int32)
        itok_B_0_15 = jax.random.randint(jax.random.fold_in(_rk, 14), (128,), 0, 16, jnp.int32)
        return (x, itok_B_0_7, itok_B_2182_4065, itok_B_0_15, _lenS)
    x, itok_B_0_7, itok_B_2182_4065, itok_B_0_15, _lenS = _rec_inputs()

    def _L0_cond_setup():
        import jax, jax.numpy as jnp
        import numpy as np
        SESSION_CHANNELS = [128, 160, 192, 224, 240, 248, 252, 64]
        N_SESS = len(SESSION_CHANNELS)
        B, MAX_C, MAX_T = (16, 64, 1024)
        HID, N_SRC = (128, 64)
        key = jax.random.key(seed)
        ks = jax.random.split(key, 7)
        session_ids = jax.random.randint(ks[0], (B,), 0, N_SESS)
        chan_table = jnp.asarray(SESSION_CHANNELS)
        channel_counts = chan_table[session_ids]
        seq_lens = jax.random.randint(ks[1], (B,), MAX_T // 2, MAX_T + 1)
        x = jax.random.normal(ks[2], (B, MAX_C, MAX_T), jnp.float32)
        cmask = (jnp.arange(MAX_C)[None, :] < channel_counts[:, None]).astype(x.dtype)
        tmask = (jnp.arange(MAX_T)[None, :] < seq_lens[:, None]).astype(x.dtype)
        x = x * cmask[:, :, None] * tmask[:, None, :]
        lim1 = 1.0 / np.sqrt(MAX_C)
        W_sess = jax.random.uniform(ks[3], (N_SESS, MAX_C, HID), jnp.float32, -lim1, lim1)
        b_sess = jax.random.uniform(ks[4], (N_SESS, HID), jnp.float32, -lim1, lim1)
        lim2 = 1.0 / np.sqrt(HID)
        W2 = jax.random.uniform(ks[5], (HID, N_SRC), jnp.float32, -lim2, lim2)
        b2 = jax.random.uniform(ks[6], (N_SRC,), jnp.float32, -lim2, lim2)
        return dict(x=x, session_ids=session_ids, channel_counts=channel_counts, seq_lens=seq_lens, W_sess=W_sess, b_sess=b_sess, W2=W2, b2=b2)
    _L0_cond_all = _L0_cond_setup()
    _L0_cond_in = {k: v for k, v in _L0_cond_all.items() if k in ('W_sess', 'b_sess', 'W2', 'b2')}
    del _L0_cond_all

    def _L0_ffn_setup():
        import jax, jax.numpy as jnp
        import numpy as np
        NUM_EXPERTS = 8
        TOP_K = 2
        RANK = 16
        LORA_ALPHA = 32
        SCALING = LORA_ALPHA / RANK
        key = jax.random.key(seed)
        ks = jax.random.split(key, 6)
        B, S, D_IN, D_OUT = (4, 512, 1024, 1024)
        x = jax.random.normal(ks[0], (B, S, D_IN), dtype=jnp.float32)
        W_base = jax.random.normal(ks[1], (D_OUT, D_IN), dtype=jnp.float32) * 0.02
        b_base = jax.random.normal(ks[2], (D_OUT,), dtype=jnp.float32) * 0.02
        W_router = jax.random.normal(ks[3], (NUM_EXPERTS, D_IN), dtype=jnp.float32) * 0.02
        A = jax.random.normal(ks[4], (NUM_EXPERTS, RANK, D_IN), dtype=jnp.float32) * 0.02
        Bm = jax.random.normal(ks[5], (D_OUT, RANK), dtype=jnp.float32) * 0.02
        Bm = jnp.broadcast_to(Bm, (NUM_EXPERTS, D_OUT, RANK)) * jnp.arange(1, NUM_EXPERTS + 1, dtype=jnp.float32)[:, None, None] * 0.2
        return {'x': x, 'W_base': W_base, 'b_base': b_base, 'W_router': W_router, 'A': A, 'B': Bm}
    _L0_ffn_all = _L0_ffn_setup()
    _L0_ffn_in = {k: v for k, v in _L0_ffn_all.items() if k in ('W_base', 'b_base', 'W_router', 'A', 'B')}
    del _L0_ffn_all

    def _L1_cond_setup():
        import jax, jax.numpy as jnp
        import numpy as np
        B, C, T = (64, 64, 1024)
        S, D = (16, 64)
        key = jax.random.key(seed)
        k1, k2, k3 = jax.random.split(key, 3)
        x = jax.random.normal(k1, (B, C, T), dtype=jnp.float32)
        condition = jax.random.randint(k2, (B,), 0, S, dtype=jnp.int64)
        bound = float(np.sqrt(6.0 / C))
        weights = jax.random.uniform(k3, (S, C, D), dtype=jnp.float32, minval=-bound, maxval=bound)
        return {'x': x, 'condition': condition, 'weights': weights}
    _L1_cond_all = _L1_cond_setup()
    _L1_cond_in = {k: v for k, v in _L1_cond_all.items() if k in ('weights',)}
    del _L1_cond_all

    def _L1_ffn_setup():
        import jax, jax.numpy as jnp
        import numpy as np
        SCALING = 16.0 / 8.0
        GAMMA = 1.0
        EPS = 1e-12
        key = jax.random.key(seed)
        ks = jax.random.split(key, 8)
        B, T, H, O = (4, 512, 1024, 1024)
        E_tot, E_act, r = (16, 4, 8)
        return {'x': jax.random.normal(ks[0], (B, T, H), jnp.float32), 'W_base': jax.random.normal(ks[1], (O, H), jnp.float32) * 0.02, 'b_base': jax.random.normal(ks[2], (O,), jnp.float32) * 0.02, 'lora_A': jax.random.normal(ks[3], (E_tot, r, H), jnp.float32) * 0.02, 'lora_B': jax.random.normal(ks[4], (E_tot, O, r), jnp.float32) * 0.02, 'router_W': jax.random.normal(ks[5], (E_tot, H), jnp.float32) * 0.02, 'router_b': jax.random.normal(ks[6], (E_tot,), jnp.float32) * 0.02, 'domain_prior': jax.random.uniform(ks[7], (E_tot,), jnp.float32), 'active': jnp.arange(E_act, dtype=jnp.int32)}
    _L1_ffn_all = _L1_ffn_setup()
    _L1_ffn_in = {k: v for k, v in _L1_ffn_all.items() if k in ('W_base', 'b_base', 'lora_A', 'lora_B', 'router_W', 'router_b', 'domain_prior', 'active')}
    del _L1_ffn_all
    return {'x': x, 'itok_B_0_7': itok_B_0_7, 'itok_B_2182_4065': itok_B_2182_4065, 'itok_B_0_15': itok_B_0_15, '_lenS': _lenS, 'L0_cond_W_sess': _L0_cond_in['W_sess'], 'L0_cond_b_sess': _L0_cond_in['b_sess'], 'L0_cond_W2': _L0_cond_in['W2'], 'L0_cond_b2': _L0_cond_in['b2'], 'L0_ffn_W_base': _L0_ffn_in['W_base'], 'L0_ffn_b_base': _L0_ffn_in['b_base'], 'L0_ffn_W_router': _L0_ffn_in['W_router'], 'L0_ffn_A': _L0_ffn_in['A'], 'L0_ffn_B': _L0_ffn_in['B'], 'L1_cond_weights': _L1_cond_in['weights'], 'L1_ffn_W_base': _L1_ffn_in['W_base'], 'L1_ffn_b_base': _L1_ffn_in['b_base'], 'L1_ffn_lora_A': _L1_ffn_in['lora_A'], 'L1_ffn_lora_B': _L1_ffn_in['lora_B'], 'L1_ffn_router_W': _L1_ffn_in['router_W'], 'L1_ffn_router_b': _L1_ffn_in['router_b'], 'L1_ffn_domain_prior': _L1_ffn_in['domain_prior'], 'L1_ffn_active': _L1_ffn_in['active']}

def reference(x, itok_B_0_7, itok_B_2182_4065, itok_B_0_15, _lenS, L0_cond_W_sess, L0_cond_b_sess, L0_cond_W2, L0_cond_b2, L0_ffn_W_base, L0_ffn_b_base, L0_ffn_W_router, L0_ffn_A, L0_ffn_B, L1_cond_weights, L1_ffn_W_base, L1_ffn_b_base, L1_ffn_lora_A, L1_ffn_lora_B, L1_ffn_router_W, L1_ffn_router_b, L1_ffn_domain_prior, L1_ffn_active):
    import jax
    import jax.numpy as jnp

    def _L0_cond_ref(x, session_ids, channel_counts, seq_lens, W_sess, b_sess, W2, b2):
        import jax, jax.numpy as jnp
        import numpy as np
        SESSION_CHANNELS = [128, 160, 192, 224, 240, 248, 252, 64]
        N_SESS = len(SESSION_CHANNELS)
        B, MAX_C, MAX_T = (16, 64, 1024)
        HID, N_SRC = (128, 64)
        cmask = (jnp.arange(x.shape[1])[None, :] < channel_counts[:, None]).astype(x.dtype)
        xm = x * cmask[:, :, None]
        W = W_sess[session_ids]
        b = b_sess[session_ids]
        h = jnp.einsum('bct,bch->bht', xm, W) + b[:, :, None]
        h = jax.nn.gelu(h, approximate=False)
        out = jnp.einsum('bht,hs->bst', h, W2) + b2[None, :, None]
        tmask = (jnp.arange(x.shape[2])[None, :] < seq_lens[:, None]).astype(x.dtype)
        return out * tmask[:, None, :]

    def _L0_ffn_ref(x, W_base, b_base, W_router, A, B):
        import jax, jax.numpy as jnp
        import numpy as np
        NUM_EXPERTS = 8
        TOP_K = 2
        RANK = 16
        LORA_ALPHA = 32
        SCALING = LORA_ALPHA / RANK
        bs, seq, d_in = x.shape
        T = bs * seq
        xf = x.reshape(T, d_in)
        base = xf @ W_base.T + b_base
        logits = xf @ W_router.T
        rw, sel = jax.lax.top_k(logits, TOP_K)
        rw = jax.nn.softmax(rw, axis=-1)
        onehot = jax.nn.one_hot(sel, NUM_EXPERTS, dtype=rw.dtype)
        w = jnp.einsum('tk,tke->te', rw, onehot)
        h = jnp.einsum('td,erd->ter', xf, A)
        lora = jnp.einsum('ter,te,eor->to', h, w, B) * SCALING
        return (base + lora).reshape(bs, seq, -1)

    def _L1_cond_ref(x, condition, weights):
        import jax, jax.numpy as jnp
        import numpy as np
        B, C, T = (64, 64, 1024)
        S, D = (16, 64)
        W = weights[condition]
        return jnp.einsum('bct,bcd->bdt', x, W)

    def _L1_ffn_ref(x, W_base, b_base, lora_A, lora_B, router_W, router_b, domain_prior, active):
        import jax, jax.numpy as jnp
        import numpy as np
        SCALING = 16.0 / 8.0
        GAMMA = 1.0
        EPS = 1e-12
        y = jnp.einsum('bth,oh->bto', x, W_base) + b_base
        A = lora_A[active]
        Bm = lora_B[active]
        z = jnp.einsum('bth,erh->bter', x, A)
        contribs = jnp.einsum('bter,eor->bteo', z, Bm) * SCALING
        logits = jnp.einsum('bth,eh->bte', x, router_W) + router_b
        logits = logits[..., active]
        prior = domain_prior[active]
        alpha = jax.nn.softmax(jnp.log(prior + EPS) + logits / GAMMA, axis=-1)
        return y + jnp.einsum('bteo,bte->bto', contribs, alpha)
    x = x + _L0_ffn_ref(_L0_cond_ref(x, itok_B_0_7, _lenS, itok_B_2182_4065, L0_cond_W_sess, L0_cond_b_sess, L0_cond_W2, L0_cond_b2), L0_ffn_W_base, L0_ffn_b_base, L0_ffn_W_router, L0_ffn_A, L0_ffn_B)
    x = x + _L1_ffn_ref(_L1_cond_ref(x, itok_B_0_15, L1_cond_weights), L1_ffn_W_base, L1_ffn_b_base, L1_ffn_lora_A, L1_ffn_lora_B, L1_ffn_router_W, L1_ffn_router_b, L1_ffn_domain_prior, L1_ffn_active)
    return x

_drawn_inputs = setup_inputs


def setup_inputs(seed=0):
    import zlib

    import numpy as np

    out = dict(_drawn_inputs(seed))
    spreads = {}
    factors = {'L0_cond_b_sess': 2.935,
     'L0_ffn_W_router': 4.393,
     'L0_ffn_A': 4.05,
     'L0_ffn_B': 4.064,
     'L1_ffn_b_base': 3.193,
     'L1_ffn_router_b': 64.0,
     'L1_ffn_domain_prior': 17.559}
    for name, (base, spread) in spreads.items():
        noise = np.random.default_rng([zlib.crc32(name.encode()), seed]).standard_normal(out[name].shape)
        drawn = base * np.exp(spread * noise) if base else spread * noise
        out[name] = jnp.asarray(drawn.astype(out[name].dtype))
    for name, factor in factors.items():
        out[name] = (out[name] * factor).astype(out[name].dtype)
    return out
```

```python
from contextlib import ExitStack

import numpy as np

import concourse.bass as bass
from concourse import mybir

F32 = mybir.dt.float32
F32R = mybir.dt.float32r
BF16 = mybir.dt.bfloat16
I32 = mybir.dt.int32
ALU = mybir.AluOpType
ACT = mybir.ActivationFunctionType
AX_X = mybir.AxisListType.X

P = 128
B, C, T = 128, 64, 1024
PAIR = P // C
NT = B // PAIR
O = T
KC = T // P
HALF = 512
KH = KC // 2
HID = 128
NS = 8
E0, R0 = 8, 16
ER0 = E0 * R0
X0 = ER0 + E0
NC = 16
ETOT, E1, R1 = 16, 4, 8
ER1 = E1 * R1
X1 = ER1 + E1
K1 = 3 * ER1 + 2
SCALING = 2.0
EPS = 1e-12
RING = 3
STAGES = 4

C_ID, C_RANK, C_T, C_CH, C_P, C_NLO = 0, P, P + E0, P + E0 + KC, P + E0 + KC + 1, P + E0 + KC + 2
C_ALL = C_NLO + 1


def constants():
    c = np.zeros((P, C_ALL), np.float32)
    p = np.arange(P)
    c[:, C_ID:C_ID + P] = np.eye(P)
    c[:, C_RANK:C_RANK + E0] = E0 - np.arange(E0)
    c[:, C_T:C_T + KC] = p[:, None] + P * np.arange(KC)
    c[:, C_CH] = p % C
    c[:, C_P] = p
    c[:, C_NLO] = -1.0 * ((p >= 2 * ER1) & (p != 3 * ER1))
    return c


class Step:

    def __init__(self, q, phase):
        self.q, self.phase = q, phase
        self.i = q * RING + phase

    def slot(self, d):
        return (self.phase + d) % RING

    def round(self, d):
        return self.q + (self.phase + d) // RING


def at_step(i):
    return Step(i // RING, i % RING)


def build(nc, d, out):
    ctx = ExitStack()
    with ctx:
        def sb(name, shape, dt=F32):
            return ctx.enter_context(nc.sbuf_tensor(name, shape, dt))

        def pb(name):
            return ctx.enter_context(nc.psum_tensor(name, [P, HALF], F32))

        def sem(name):
            return ctx.enter_context(nc.semaphore(name))

        def f32(ap):
            return ap.bitcast(F32)

        w0 = [sb(f"w0_{s}", [P, KC, O], F32R) for s in ("hi", "lo")]
        w1 = [sb(f"w1_{s}", [P, KC, O], F32R) for s in ("hi", "lo")]
        a0 = [sb(f"a0_{s}", [P, KC, X0], F32R) for s in ("hi", "lo")]
        a1 = [sb(f"a1_{s}", [P, KC, X1], F32R) for s in ("hi", "lo")]
        b0t = [sb(f"b0t_{s}", [ER0, O], F32R) for s in ("hi", "lo")]
        b1s = sb("b1_stack", [K1, O], F32R)
        w2 = [sb(f"w2_{s}", [HID, C], F32R) for s in ("hi", "lo")]
        const = sb("const", [P, C_ALL])
        ident = const[:, C_ID:C_ID + P]
        rank = const[:, C_RANK:C_RANK + E0]
        w2raw = sb("w2_raw", [HID, C])
        b2bc = sb("b2_bc", [P, C])
        b0bc = sb("b0_bc", [P, O])
        sess_bias = sb("sess_bias", [HID, B])
        hbias = sb("hid_bias", [HID, PAIR])
        bsess = sb("b_sess", [NS, HID])
        onehot = sb("onehot", [NS, B])
        tmask = sb("tmask", [P, NT, KC * PAIR], BF16)
        cmask = sb("cmask", [P, NT])
        ids = sb("ids", [1, 2 * B + E1], I32)
        lens = sb("lens", [P, NT], I32)
        sess8 = sb("sess8", [NS, B], I32)
        seqs = sb("seqs", [P, B], I32)
        prior = sb("prior", [P, E1])
        rbias = sb("rbias", [P, E1])
        logit_bias = sb("logit_bias", [P, E1])
        xr = sb("x_ring", [P, RING, T])
        xs = [sb(f"xs_{s}", [P, T], F32R) for s in ("hi", "lo")]
        tmp = sb("tmp", [P, PAIR * HALF])
        g = [sb(f"g_{s}", [HID, PAIR, HALF], F32R) for s in ("hi", "lo")]
        c0 = [sb(f"c0_{s}", [P, KC, P], F32R) for s in ("hi", "lo")]
        c1 = [sb(f"c1_{s}", [P, KC, P], F32R) for s in ("hi", "lo")]
        wraw = sb("wsess_raw", [P, HID])
        ws = [sb(f"ws_{s}", [P, HID], F32R) for s in ("hi", "lo")]
        vraw = sb("v_raw", [P, P])
        vs = [sb(f"vs_{s}", [P, P], F32R) for s in ("hi", "lo")]
        lg = sb("lg", [P, E0])
        top = sb("top", [P, 8])
        pick = [sb(f"pick{j}", [P, E0]) for j in range(2)]
        first = [sb(f"first{j}", [P, 1]) for j in range(2)]
        left = sb("left", [P, E0])
        gap = sb("gap", [P, 1])
        egap = sb("egap", [P, 1])
        esum = sb("esum", [P, 1])
        wtop = [sb(f"wtop{j}", [P, 1]) for j in range(2)]
        wsel = [sb(f"wsel{j}", [P, E0]) for j in range(2)]
        wsum = sb("wsum", [P, E0])
        hw0 = sb("hw0", [P, E0, R0])
        h0t = [sb(f"h0t_{s}", [ER0, P], F32R) for s in ("hi", "lo")]
        z1 = sb("z1", [P, E1])
        nmax = sb("nmax", [P, 1])
        ez = sb("ez", [P, E1])
        zsum = sb("zsum", [P, 1])
        zinv = sb("zinv", [P, 1])
        alpha = sb("alpha", [P, E1])
        hw1 = sb("hw1", [P, E1, R1])
        h1s = sb("h1_stack", [P, K1], F32R)
        h1t = sb("h1t", [K1, P], F32R)

        psM = [pb("psM0"), pb("psM1")]
        psC = [pb("psC0"), pb("psC1")]
        psH = [pb("psH0"), pb("psH1")]
        psR = [pb("psR0"), pb("psR1")]

        setup_in = sem("setup_in")
        pick_in = sem("pick_in")
        stage_in = [sem(f"stage_in{s}") for s in range(STAGES)]
        stage_hi = sem("stage_hi")
        stage_lo = sem("stage_lo")
        v_zero = sem("v_zero")
        tables = sem("tables")
        bias_ps = sem("bias_ps")
        logits_in = sem("logits_in")
        x_in = [[sem(f"x_in{s}{h}") for h in range(2)] for s in range(RING)]
        x_out = [[sem(f"x_out{s}{h}") for h in range(2)] for s in range(RING)]
        w_in = sem("w_in")
        v_in = sem("v_in")
        ws_hi = sem("ws_hi")
        w_split = sem("w_split")
        vs_hi = sem("vs_hi")
        v_split = sem("v_split")
        xhi_h = sem("xhi_h")
        xlo_h = sem("xlo_h")
        xb_h = sem("xb_h")
        hid_h = sem("hid_h")
        gelu_h = sem("gelu_h")
        ghi_h = sem("ghi_h")
        glo_h = sem("glo_h")
        co_h = sem("co_h")
        cb_h = sem("cb_h")
        cm_h = sem("cm_h")
        c0hi_h = sem("c0hi_h")
        c0lo_h = sem("c0lo_h")
        a0_done = sem("a0_done")
        gap_done = sem("gap_done")
        egap_done = sem("egap_done")
        route0 = sem("route0")
        hw0_done = sem("hw0_done")
        t0_done = sem("t0_done")
        h0hi_done = sem("h0hi_done")
        h0lo_done = sem("h0lo_done")
        m0_h = sem("m0_h")
        x1_h = sem("x1_h")
        x1hi_h = sem("x1hi_h")
        x1lo_h = sem("x1lo_h")
        mix_h = sem("mix_h")
        c1hi_h = sem("c1hi_h")
        c1lo_h = sem("c1lo_h")
        a1_done = sem("a1_done")
        nmax_done = sem("nmax_done")
        ez_done = sem("ez_done")
        route1 = sem("route1")
        hw1_done = sem("hw1_done")
        t1_done = sem("t1_done")
        h1t_done = sem("h1t_done")
        m1_h = sem("m1_h")
        x2_h = sem("x2_h")

        stages = [xr[:, 0, :], xr[:, 1, :], xr[:, 2, :], tmp[:, :]]

        def cols(ap):
            return ap.rearrange("p a n -> p (a n)")

        pieces = []
        for k in range(2):
            ks = slice(k * KH, k * KH + KH)
            pieces.append((cols(d["a0"][:, ks, :]), cols(a0[0][:, ks, :]), cols(a0[1][:, ks, :])))
        for k in range(KC):
            pieces.append((d["w0"][k * P:(k + 1) * P, :], w0[0][:, k, :], w0[1][:, k, :]))
        pieces.append((d["b0t"], b0t[0][:, :], b0t[1][:, :]))
        for k in range(KC):
            pieces.append((d["w1"][k * P:(k + 1) * P, :], w1[0][:, k, :], w1[1][:, k, :]))
        GATHER_A, GATHER_B = len(pieces), len(pieces) + 1
        pieces.append((None, cols(a1[0][:, :, :]), cols(a1[1][:, :, :])))
        pieces.append((None, None, None))
        SETUP_IN = 16 * 10
        STAGE_GATHERS = {GATHER_A: E1, GATHER_B: 3 * E1 + 2}

        def staged(n):
            return sum(16 * STAGE_GATHERS.get(m, 1) for m in range(n % STAGES, n + 1, STAGES))

        block = ctx.enter_context(nc.Block())

        @block.sync
        def _(sp):
            def row(ap, n):
                return ap.partition_broadcast(n)

            def gather_w(s, dt):
                for b in range(PAIR):
                    n = sp.value_load(ids[0:1, bass.ds(s.i * PAIR + (PAIR * dt + b), 1)], min_val=0, max_val=NS - 1)
                    sp.dma_start(wraw[C * b:C * b + C, :],
                                 d["wsess"][bass.ds(n, 1), :, :].rearrange("a c n -> (a c) n")).then_inc(w_in, 16)

            def gather_v(s, dt):
                for b in range(PAIR):
                    n = sp.value_load(ids[0:1, bass.ds(s.i * PAIR + (B + PAIR * dt + b), 1)], min_val=0, max_val=NC - 1)
                    sp.dma_start(vraw[C * b:C * b + C, C * b:C * b + C],
                                 d["mixw"][bass.ds(n, 1), :, :].rearrange("a c n -> (a c) n")).then_inc(v_in, 16)

            def load(s, dt, h):
                hs = slice(HALF * h, HALF * h + HALF)
                sp.dma_start(xr[:, s.slot(dt), hs],
                             d["x"][bass.ds(s.i + dt, 1), :, hs].rearrange("a p n -> (a p) n")
                             ).then_inc(x_in[s.slot(dt)][h], 16)

            def store(s, dt, h):
                hs = slice(HALF * h, HALF * h + HALF)
                sp.dma_start(out[bass.ds(s.i + dt, 1), :, hs].rearrange("a p n -> (a p) n"),
                             xr[:, s.slot(dt), hs]).then_inc(x_out[s.slot(dt)][h], 16)

            def step(s, gw=True, gv=True, ld=True, st=True):
                if gw:
                    sp.wait_ge(w_split, s.i + 2)
                    gather_w(s, 2)
                if gv:
                    sp.wait_ge(v_split, s.i + 1)
                    gather_v(s, 1)
                for h in range(2):
                    if st:
                        sp.wait_ge(x2_h, s.i * 2 + (h - 1))
                        store(s, -1, h)
                    if ld:
                        if st:
                            sp.wait_ge(x_out[s.slot(2)][h], (s.round(2)) * 16)
                        load(s, 2, h)

            sp.dma_start(ids[:, :], d["ids"]).then_inc(setup_in, 16)
            sp.dma_start(const[:, :], d["const"]).then_inc(setup_in, 16)
            sp.dma_start(w2raw[:, :], d["w2"]).then_inc(setup_in, 16)
            sp.dma_start(b2bc[:, :], row(d["b2"], P)).then_inc(setup_in, 16)
            sp.dma_start(b0bc[:, :], row(d["b0"], P)).then_inc(setup_in, 16)
            sp.dma_start(bsess[:, :], d["bsess"]).then_inc(setup_in, 16)
            for b in range(PAIR):
                sp.dma_start(lens[C * b:C * b + C, :], row(d["lens"][b], C)).then_inc(setup_in, 16)
            sp.dma_start(sess8[:, :], row(d["sess"], NS)).then_inc(setup_in, 16)
            sp.dma_start(seqs[:, :], row(d["seqs"], P)).then_inc(setup_in, 16)
            sp.wait_ge(setup_in, SETUP_IN)
            active = [sp.value_load(ids[0:1, 2 * B + j:2 * B + j + 1], min_val=0, max_val=ETOT - 1)
                      for j in range(E1)]
            for j in range(E1):
                sp.dma_start(prior[:, j:j + 1], row(d["prior"][bass.ds(active[j], 1)], P)).then_inc(pick_in, 16)
                sp.dma_start(rbias[:, j:j + 1], row(d["rb"][bass.ds(active[j], 1)], P)).then_inc(pick_in, 16)
            sp.wait_ge(v_zero, 1)
            gather_w(at_step(0), 0)
            gather_v(at_step(0), 0)
            for n, (src, hi, _lo) in enumerate(pieces):
                st = stages[n % STAGES]
                if n >= STAGES:
                    sp.wait_ge(stage_lo, n - STAGES + 1)
                done = stage_in[n % STAGES]
                if src is not None:
                    sp.dma_start(st[:, 0:src.shape[1]], src).then_inc(done, 16)
                elif n == GATHER_A:
                    to = st[:, 0:KC * X1].rearrange("p (k n) -> p k n", k=KC)
                    for j in range(E1):
                        one = bass.ds(active[j], 1)
                        sp.dma_start(to[:, :, (R1 + 1) * j:(R1 + 1) * (j + 1)],
                                     d["a1"][one, :, :, :].rearrange("a p k r -> (a p) k r")).then_inc(done, 16)
                else:
                    for rep in range(3):
                        for j in range(E1):
                            r = rep * ER1 + R1 * j
                            sp.dma_start(st[r:r + R1, :], d["b1t"][bass.ds(active[j], 1), :, :]
                                         .rearrange("a r n -> (a r) n")).then_inc(done, 16)
                    for r in range(2):
                        sp.dma_start(st[3 * ER1 + r:3 * ER1 + r + 1, :], d["b1"]).then_inc(done, 16)
            sp.wait_ge(stage_lo, len(pieces))
            for dt in range(2):
                for h in range(2):
                    load(at_step(0), dt, h)
            sp.wait_ge(w_split, 1)
            gather_w(at_step(0), 1)
            step(at_step(0), st=False)
            with sp.Fori(0, (NT - 4) // RING) as q:
                for u in range(RING):
                    step(Step(q, 1 + u))
            step(at_step(NT - 3))
            step(at_step(NT - 2), gw=False, ld=False)
            step(at_step(NT - 1), gw=False, gv=False, ld=False)
            step(at_step(NT), gw=False, gv=False, ld=False)
            for s in range(RING):
                for h in range(2):
                    sp.wait_ge(x_out[s][h], 16 * len(range(s, NT, RING)))

        @block.tensor
        def _(pe):
            def three(out_, left_, right_, start=True, stop=True):
                nc.tensor.matmul(out_, left_[0], right_[0], start=start, stop=False)
                nc.tensor.matmul(out_, left_[0], right_[1], start=False, stop=False)
                return nc.tensor.matmul(out_, left_[1], right_[0], start=False, stop=stop)

            def hidden(i, h):
                pe.wait_ge(xlo_h, i * 2 + (h + 1))
                if h == 0:
                    pe.wait_ge(w_split, i + 1)
                if h or not (isinstance(i, int) and i == 0):
                    pe.wait_ge(gelu_h, i * 2 + h)
                hs = slice(HALF * h, HALF * h + HALF)
                for j, (a, b) in enumerate(((0, 0), (0, 1), (1, 0))):
                    for bt in range(PAIR):
                        r = slice(C * bt, C * bt + C)
                        last = nc.tensor.matmul(psH[bt][:, :], ws[a][r, :], xs[b][r, hs],
                                                start=(j == 0), stop=(j == 2))
                last.then_inc(hid_h, 1)

            def cond0(i, h, early=False):
                pe.wait_ge(glo_h, i * 2 + (h + 1))
                if not early:
                    pe.wait_ge(c1lo_h, i * 2 + (h - 3))
                for k in range(KH):
                    for bt in range(PAIR):
                        at = k * P + bt * C
                        last = three(psC[h][:, at:at + C], [t[:, bt, k * P:(k + 1) * P] for t in g],
                                     [t[:, :] for t in w2])
                last.then_inc(co_h, 1)

            def low(x, a, ps, n):
                for k in range(KC):
                    last = three(ps[:, 0:n], [t[:, k, :] for t in x], [t[:, k, :] for t in a],
                                 start=(k == 0), stop=(k == KC - 1))
                return last

            def ffn(x, w, h, ks):
                for k in ks:
                    three(psM[h][:, :], [t[:, k, :] for t in x],
                          [t[:, k, HALF * h:HALF * h + HALF] for t in w], start=(k == 0), stop=False)

            def step(i, prep=True, l0=True, l1=True, early=False):
                if l0:
                    pe.wait_ge(c0lo_h, i * 2 + 2)
                    low(c0, a0, psR[0], X0).then_inc(a0_done, 1)
                    if l1 and not early:
                        pe.wait_ge(x2_h, i * 2 - 3)
                    ffn(c0, w0, 0, range(6))
                    pe.wait_ge(hw0_done, i + 1)
                    nc.tensor.transpose(psR[0][:, 2 * P:3 * P], hw0[:, :, :].rearrange("p e r -> p (e r)"),
                                        ident).then_inc(t0_done, 1)
                    if prep:
                        hidden(i + 1, 0)
                    ffn(c0, w0, 0, range(6, KC))
                    pe.wait_ge(h0lo_done, i + 1)
                    three(psM[0][:, :], [t[:, :] for t in h0t], [t[:, 0:HALF] for t in b0t],
                          start=False).then_inc(m0_h, 1)
                    if l1 and not early:
                        pe.wait_ge(x2_h, i * 2 - 2)
                    ffn(c0, w0, 1, range(3))
                    if prep:
                        cond0(i + 1, 0, early=not l1)
                        hidden(i + 1, 1)
                    ffn(c0, w0, 1, range(3, KC))
                    three(psM[1][:, :], [t[:, :] for t in h0t], [t[:, HALF:O] for t in b0t],
                          start=False).then_inc(m0_h, 1)
                if l1:
                    pe.wait_ge(c1lo_h, i * 2)
                    low(c1, a1, psR[1], X1).then_inc(a1_done, 1)
                    if l0:
                        pe.wait_ge(x1_h, i * 2 + 1)
                    else:
                        pe.wait_ge(x2_h, i * 2 - 3)
                    ffn(c1, w1, 0, range(4))
                if l0 and prep:
                    cond0(i + 1, 1, early=not l1)
                if l1:
                    ffn(c1, w1, 0, range(4, 7))
                    pe.wait_ge(hw1_done, i)
                    nc.tensor.transpose(psR[1][0:K1, 2 * P:3 * P], f32(h1s[:, :]), ident).then_inc(t1_done, 1)
                    ffn(c1, w1, 0, range(7, KC))
                    pe.wait_ge(h1t_done, i)
                    for h in range(2):
                        if h == 1:
                            if l0:
                                pe.wait_ge(x1_h, i * 2 + 2)
                            else:
                                pe.wait_ge(x2_h, i * 2 - 2)
                            ffn(c1, w1, 1, range(KC))
                        nc.tensor.matmul(psM[h][:, :], h1t[:, :], b1s[:, HALF * h:HALF * h + HALF],
                                         start=False, stop=True).then_inc(m1_h, 1)
                if l0:
                    pe.wait_ge(v_split, i + 1)
                    for h in range(2):
                        pe.wait_ge(x1lo_h, i * 2 + (h + 1))
                        if prep:
                            pe.wait_ge(cb_h, i * 2 + (h + 3))
                        for k in range(KH):
                            at = slice((KH * h + k) * P, (KH * h + k + 1) * P)
                            last = three(psC[h][:, k * P:(k + 1) * P], [t[:, at] for t in xs],
                                         [t[:, :] for t in vs])
                        last.then_inc(mix_h, 1)

            pe.wait_ge(tables, 1)
            pe.wait_ge(setup_in, SETUP_IN)
            nc.tensor.matmul(psR[0][:, 0:B], bsess[:, :], onehot[:, :], start=True, stop=True).then_inc(bias_ps, 1)
            pe.wait_ge(stage_lo, len(pieces))
            for h in range(2):
                hidden(0, h)
                cond0(0, h, early=True)
            step(0, l1=False)
            step(1, early=True)
            with pe.Fori(2, NT - 1) as i:
                step(i)
            step(NT - 1, prep=False)
            step(NT, prep=False, l0=False)

        @block.scalar
        def _(act):
            def hi(out_, in_):
                return nc.scalar.activation(out_, in_, ACT.Copy)

            def split_x(s, dt, h):
                hs = slice(HALF * h, HALF * h + HALF)
                act.wait_ge(x_in[s.slot(dt)][h], s.round(dt) * 16 + 16)
                hi(xs[0][:, hs], xr[:, s.slot(dt), hs]).then_inc(xhi_h, 1)

            def hidden(s, dt, h, first=False):
                i = s.i + dt
                act.wait_ge(hid_h, i * 2 + (h + 1))
                if h:
                    act.wait_ge(glo_h, i * 2 + h)
                elif not first:
                    act.wait_ge(c0lo_h, i * 2)
                for bt in range(PAIR):
                    last = nc.scalar.activation(tmp[:, bt * HALF:(bt + 1) * HALF], psH[bt][:, :], ACT.Gelu,
                                                bias=hbias[:, bt:bt + 1])
                last.then_inc(gelu_h, 1)
                act.wait_ge(gelu_h, i * 2 + (h + 1))
                hi(g[0][:, :, :].rearrange("p b n -> p (b n)"), tmp[:, :]).then_inc(ghi_h, 1)

            def split_c0(i, h):
                act.wait_ge(cm_h, i * 2 + (h + 1))
                hi(c0[0][:, KH * h:KH * h + KH, :].rearrange("p k n -> p (k n)"),
                   tmp[:, HALF * h:HALF * h + HALF]).then_inc(c0hi_h, 1)

            def step(s, prep=True, l0=True, l1=True, early=False):
                i = s.i
                if l1:
                    if not early:
                        act.wait_ge(m1_h, i * 2 - 2)
                    for h in range(2):
                        act.wait_ge(mix_h, i * 2 + (h - 1))
                        hi(c1[0][:, KH * h:KH * h + KH, :].rearrange("p k n -> p (k n)"),
                           psC[h][:, :]).then_inc(c1hi_h, 1)
                if prep:
                    split_x(s, 1, 0)
                if l0:
                    act.wait_ge(gap_done, i + 1)
                    nc.scalar.activation(egap[:, :], gap[:, :], ACT.Exp).then_inc(egap_done, 1)
                if prep:
                    split_x(s, 1, 1)
                if l0:
                    act.wait_ge(t0_done, i + 1)
                    hi(h0t[0][:, :], psR[0][:, 2 * P:3 * P]).then_inc(h0hi_done, 1)
                if prep:
                    for h in range(2):
                        hidden(s, 1, h)
                if l0:
                    for h in range(2):
                        hs = slice(HALF * h, HALF * h + HALF)
                        act.wait_ge(x1_h, i * 2 + (h + 1))
                        hi(xs[0][:, hs], xr[:, s.slot(0), hs]).then_inc(x1hi_h, 1)
                if l1:
                    act.wait_ge(nmax_done, i)
                    nc.scalar.activation(ez[:, :], z1[:, :], ACT.Exp, bias=nmax[:, 0:1],
                                         accum_out=zsum[:, :]).then_inc(ez_done, 1)
                    act.wait_ge(t1_done, i)
                    hi(h1t[:, :], psR[1][0:K1, 2 * P:3 * P]).then_inc(h1t_done, 1)
                if prep:
                    act.wait_ge(m0_h, i * 2 + 2)
                    for h in range(2):
                        split_c0(i + 1, h)

            act.wait_ge(tables, 2)
            nc.scalar.activation(prior[:, :], prior[:, :], ACT.Ln).then_inc(logits_in, 1)
            act.wait_ge(setup_in, SETUP_IN)
            hi(w2[0][:, :], w2raw[:, :]).then_inc(stage_hi, 1)
            for n, (src, hi_, _lo) in enumerate(pieces):
                act.wait_ge(stage_in[n % STAGES], staged(n))
                if n == GATHER_B:
                    hi(b1s[:, :], stages[n % STAGES][0:K1, :]).then_inc(stage_hi, 1)
                else:
                    hi(hi_, stages[n % STAGES][:, 0:hi_.shape[1]]).then_inc(stage_hi, 1)
            for h in range(2):
                split_x(at_step(0), 0, h)
            act.wait_ge(tables, 4)
            for h in range(2):
                hidden(at_step(0), 0, h, first=True)
            for h in range(2):
                split_c0(0, h)
            step(at_step(0), l1=False)
            step(at_step(1), early=True)
            step(at_step(2))
            step(at_step(3))
            with act.Fori(1, NT // RING - 1) as q:
                for u in range(RING):
                    step(Step(q, 1 + u))
            for i in range(RING * (NT // RING - 1) + 1, NT - 1):
                step(at_step(i))
            step(at_step(NT - 1), prep=False)
            step(at_step(NT), prep=False, l0=False)

        @block.vector
        def _(dve):
            tt, ts, stt = nc.vector.tensor_tensor, nc.vector.tensor_scalar, nc.vector.scalar_tensor_tensor

            def lo(out_, in_, hi_):
                return tt(out_, in_, f32(hi_), ALU.subtract)

            def split_w(i, first=False):
                dve.wait_ge(w_in, i * (16 * PAIR) + 16 * PAIR)
                if not first:
                    dve.wait_ge(hid_h, i * 2)
                cm = cmask[:, bass.ds(i, 1)]
                ts(hbias[:, :], sess_bias[:, bass.ds(i * PAIR, PAIR)], 1.0, None, ALU.mult)
                ts(ws[0][:, :], wraw[:, :], cm, None, ALU.mult).then_inc(ws_hi, 1)
                dve.wait_ge(ws_hi, i + 1)
                stt(ws[1][:, :], wraw[:, :], cm, f32(ws[0][:, :]), ALU.mult, ALU.subtract).then_inc(w_split, 1)

            def split_v(i):
                dve.wait_ge(v_in, i * (16 * PAIR) + 16 * PAIR)
                nc.vector.tensor_copy(vs[0][:, :], vraw[:, :]).then_inc(vs_hi, 1)
                dve.wait_ge(vs_hi, i + 1)
                lo(vs[1][:, :], vraw[:, :], vs[0][:, :]).then_inc(v_split, 1)

            def split_x(s, dt, h):
                hs = slice(HALF * h, HALF * h + HALF)
                dve.wait_ge(xhi_h, s.i * 2 + (2 * dt + h + 1))
                lo(xs[1][:, hs], xr[:, s.slot(dt), hs], xs[0][:, hs]).then_inc(xlo_h, 1)

            def split_g(i, h):
                dve.wait_ge(ghi_h, i * 2 + (h + 1))
                lo(g[1][:, :, :].rearrange("p b n -> p (b n)"), tmp[:, :],
                   g[0][:, :, :].rearrange("p b n -> p (b n)")).then_inc(glo_h, 1)

            def bias_c0(i, h):
                dve.wait_ge(co_h, i * 2 + (h + 1))
                dve.wait_ge(glo_h, i * 2 + 2)
                t = tmp[:, HALF * h:HALF * h + HALF].rearrange("p (m s) -> p m s", s=C)
                tt(t, psC[h][:, :].rearrange("p (m s) -> p m s", s=C),
                   b2bc[:, :].unsqueeze(1).to_broadcast([P, HALF // C, C]), ALU.add).then_inc(cb_h, 1)

            def split_c0(i, h):
                dve.wait_ge(c0hi_h, i * 2 + (h + 1))
                t = slice(KH * h, KH * h + KH)
                lo(c0[1][:, t, :].rearrange("p k n -> p (k n)"), tmp[:, HALF * h:HALF * h + HALF],
                   c0[0][:, t, :].rearrange("p k n -> p (k n)")).then_inc(c0lo_h, 1)

            ROUTE0, ROUTE1 = 13, 5

            def route_0(i):
                done = [0]

                def link(ins, sync=True):
                    done[0] += 1
                    ins.then_inc(route0, 1)
                    if sync:
                        dve.wait_ge(route0, i * ROUTE0 + done[0])

                dve.wait_ge(a0_done, i + 1)
                link(nc.vector.tensor_copy(lg[:, :], psR[0][:, ER0:X0]), sync=False)
                link(nc.vector.max(top[:, :], psR[0][:, ER0:X0]))
                tt(gap[:, :], top[:, 1:2], top[:, 0:1], ALU.subtract).then_inc(gap_done, 1)
                link(stt(pick[0][:, :], lg[:, :], top[:, 0:1], rank, ALU.is_equal, ALU.mult))
                link(nc.vector.tensor_reduce(first[0][:, :], pick[0][:, :], AX_X, ALU.max))
                link(stt(left[:, :], rank, first[0][:, 0:1], rank, ALU.not_equal, ALU.mult))
                link(stt(pick[1][:, :], lg[:, :], top[:, 1:2], left[:, :], ALU.is_equal, ALU.mult))
                link(nc.vector.tensor_reduce(first[1][:, :], pick[1][:, :], AX_X, ALU.max), sync=False)
                dve.wait_ge(egap_done, i + 1)
                link(ts(esum[:, :], egap[:, :], 1.0, 1.0 / SCALING, ALU.add, ALU.mult))
                link(nc.vector.reciprocal(wtop[0][:, :], esum[:, :]))
                link(ts(wtop[1][:, :], egap[:, :], wtop[0][:, 0:1], None, ALU.mult), sync=False)
                link(ts(wsel[0][:, :], rank, first[0][:, 0:1], wtop[0][:, 0:1], ALU.is_equal, ALU.mult))
                link(ts(wsel[1][:, :], rank, first[1][:, 0:1], wtop[1][:, 0:1], ALU.is_equal, ALU.mult))
                link(tt(wsum[:, :], wsel[0][:, :], wsel[1][:, :], ALU.add))
                assert done[0] == ROUTE0
                tt(hw0[:, :, :], psR[0][:, 0:ER0].rearrange("p (e r) -> p e r", e=E0),
                   wsum[:, :].unsqueeze(2).to_broadcast([P, E0, R0]), ALU.mult).then_inc(hw0_done, 1)

            def route_1(i):
                done = [0]

                def link(ins):
                    done[0] += 1
                    ins.then_inc(route1, 1)
                    dve.wait_ge(route1, i * ROUTE1 + done[0])

                dve.wait_ge(a1_done, i + 1)
                out1 = psR[1][:, 0:X1].rearrange("p (e r) -> p e r", e=E1)
                link(tt(z1[:, :], out1[:, :, R1:R1 + 1].rearrange("p e r -> p (e r)"), logit_bias[:, :], ALU.add))
                nc.vector.tensor_reduce(nmax[:, :], z1[:, :], AX_X, ALU.max, negate=True).then_inc(nmax_done, 1)
                dve.wait_ge(ez_done, i + 1)
                link(nc.vector.reciprocal(zinv[:, :], zsum[:, :]))
                link(ts(alpha[:, :], ez[:, :], zinv[:, 0:1], SCALING, ALU.mult, ALU.mult))
                link(tt(hw1[:, :, :], out1[:, :, 0:R1],
                        alpha[:, :].unsqueeze(2).to_broadcast([P, E1, R1]), ALU.mult))
                hw = hw1[:, :, :].rearrange("p e r -> p (e r)")
                link(nc.vector.tensor_copy(h1s[:, 0:ER1], hw))
                assert done[0] == ROUTE1
                nc.vector.tensor_copy(h1s[:, 2 * ER1:3 * ER1], hw)
                lo(h1s[:, ER1:2 * ER1], hw, h1s[:, 0:ER1]).then_inc(hw1_done, 1)

            def step(s, prep=True, l0=True, l1=True):
                i = s.i
                if l1:
                    for h in range(2):
                        t = slice(KH * h, KH * h + KH)
                        dve.wait_ge(c1hi_h, i * 2 + (h - 1))
                        lo(c1[1][:, t, :].rearrange("p k n -> p (k n)"), psC[h][:, :],
                           c1[0][:, t, :].rearrange("p k n -> p (k n)")).then_inc(c1lo_h, 1)
                if prep:
                    split_w(i + 1)
                if l0:
                    split_v(i)
                if prep:
                    split_x(s, 1, 0)
                if l0:
                    route_0(i)
                if prep:
                    split_x(s, 1, 1)
                if l0:
                    dve.wait_ge(h0hi_done, i + 1)
                    lo(h0t[1][:, :], psR[0][:, 2 * P:3 * P], h0t[0][:, :]).then_inc(h0lo_done, 1)
                for h in range(2):
                    hs = slice(HALF * h, HALF * h + HALF)
                    if prep:
                        split_g(i + 1, h)
                    if l0:
                        dve.wait_ge(m0_h, i * 2 + (h + 1))
                        dve.wait_ge(xb_h, i * 2 + (h + 1))
                        tt(xr[:, s.slot(0), hs], xr[:, s.slot(0), hs], psM[h][:, :], ALU.add).then_inc(x1_h, 1)
                if l0:
                    for h in range(2):
                        hs = slice(HALF * h, HALF * h + HALF)
                        dve.wait_ge(x1hi_h, i * 2 + (h + 1))
                        lo(xs[1][:, hs], xr[:, s.slot(0), hs], xs[0][:, hs]).then_inc(x1lo_h, 1)
                if l1:
                    route_1(i - 1)
                if prep:
                    for h in range(2):
                        bias_c0(i + 1, h)
                    for h in range(2):
                        split_c0(i + 1, h)
                if l1:
                    for h in range(2):
                        hs = slice(HALF * h, HALF * h + HALF)
                        dve.wait_ge(m1_h, i * 2 + (h - 1))
                        tt(xr[:, s.slot(-1), hs], xr[:, s.slot(-1), hs], psM[h][:, :], ALU.add).then_inc(x2_h, 1)

            nc.vector.memset(vraw[:, :], 0.0).then_inc(v_zero, 1)
            dve.wait_ge(setup_in, SETUP_IN)
            ts(onehot[:, :], sess8[:, :], const[0:NS, C_P:C_P + 1], None, ALU.is_equal).then_inc(tables, 1)
            dve.wait_ge(pick_in, 16 * 2 * E1)
            ts(prior[:, :], prior[:, :], EPS, None, ALU.add).then_inc(tables, 1)
            ts(cmask[:, :], lens[:, :], const[:, C_CH:C_CH + 1], None, ALU.is_gt)
            m = tmask[:, :, :].rearrange("p n (k b) -> p n k b", b=PAIR)
            for k in range(KC):
                last = ts(m[:, :, k, :], seqs[:, :].rearrange("p (n b) -> p n b", b=PAIR),
                          const[:, C_T + k:C_T + k + 1], None, ALU.is_gt)
            nc.vector.memset(f32(h1s[:, 3 * ER1:K1]), 1.0)
            last.then_inc(tables, 1)
            dve.wait_ge(tables, 3)
            dve.wait_ge(bias_ps, 1)
            nc.vector.tensor_copy(sess_bias[:, :], psR[0][:, 0:B]).then_inc(tables, 1)
            dve.wait_ge(logits_in, 1)
            tt(logit_bias[:, :], prior[:, :], rbias[:, :], ALU.add)
            dve.wait_ge(stage_hi, 1)
            lo(w2[1][:, :], w2raw[:, :], w2[0][:, :])
            for n, (src, hi_, lo_) in enumerate(pieces):
                dve.wait_ge(stage_hi, n + 2)
                st = stages[n % STAGES]
                if n == GATHER_B:
                    r = slice(2 * ER1, K1)
                    stt(b1s[r, :], f32(b1s[r, :]), const[r, C_NLO:C_NLO + 1], st[r, :],
                        ALU.mult, ALU.add).then_inc(stage_lo, 1)
                else:
                    lo(lo_, st[:, 0:lo_.shape[1]], hi_).then_inc(stage_lo, 1)
            split_w(0, first=True)
            s = at_step(0)
            for h in range(2):
                split_x(s, 0, h)
            for h in range(2):
                split_g(0, h)
            for h in range(2):
                bias_c0(0, h)
            for h in range(2):
                split_c0(0, h)
            step(at_step(0), l1=False)
            with dve.Fori(0, NT // RING - 1) as q:
                for u in range(RING):
                    step(Step(q, 1 + u))
            for i in range(RING * (NT // RING - 1) + 1, NT - 1):
                step(at_step(i))
            step(at_step(NT - 1), prep=False)
            step(at_step(NT), prep=False, l0=False)

        @block.gpsimd
        def _(pool):
            def bias_x(s, dt, h):
                hs = slice(HALF * h, HALF * h + HALF)
                pool.wait_ge(xlo_h, s.i * 2 + (2 * dt + h + 1))
                nc.gpsimd.tensor_tensor(xr[:, s.slot(dt), hs], xr[:, s.slot(dt), hs], b0bc[:, hs],
                                        ALU.add).then_inc(xb_h, 1)

            def mask(i, h):
                pool.wait_ge(cb_h, i * 2 + (h + 1))
                t = tmp[:, HALF * h:HALF * h + HALF].rearrange("p (m s) -> p m s", s=C)
                m = tmask[:, bass.ds(i, 1), h * (HALF // C):(h + 1) * (HALF // C)].rearrange("p a m -> p (a m)")
                nc.gpsimd.tensor_tensor(t, t, m.unsqueeze(2).to_broadcast([P, HALF // C, C]),
                                        ALU.mult).then_inc(cm_h, 1)

            def step(s):
                for h in range(2):
                    bias_x(s, 1, h)
                for h in range(2):
                    mask(s.i + 1, h)

            pool.wait_ge(setup_in, SETUP_IN)
            pool.wait_ge(tables, 3)
            for h in range(2):
                bias_x(at_step(0), 0, h)
            for h in range(2):
                mask(0, h)
            step(at_step(0))
            with pool.Fori(0, NT // RING - 1) as q:
                for u in range(RING):
                    step(Step(q, 1 + u))
            for i in range(RING * (NT // RING - 1) + 1, NT - 1):
                step(at_step(i))


def kernel(**inputs):
    import concourse.bacc as bacc
    from concourse.bass_utils import run_bass_kernel_spmd

    a = {k: np.ascontiguousarray(v) for k, v in inputs.items()}
    sess, seqs, cond, lens = a["itok_B_0_7"], a["itok_B_2182_4065"], a["itok_B_0_15"], a["_lenS"]
    laid = {
        "x": a["x"].reshape(NT, P, T),
        "ids": np.concatenate([sess, cond, a["L1_ffn_active"]])[None, :],
        "lens": lens.reshape(NT, PAIR).T,
        "sess": sess,
        "seqs": seqs,
        "const": constants(),
        "wsess": a["L0_cond_W_sess"],
        "bsess": a["L0_cond_b_sess"],
        "w2": a["L0_cond_W2"],
        "b2": a["L0_cond_b2"],
        "w0": a["L0_ffn_W_base"].T,
        "b0": a["L0_ffn_b_base"],
        "a0": np.concatenate([a["L0_ffn_A"].reshape(ER0, T), a["L0_ffn_W_router"]]).T
              .reshape(KC, P, X0).transpose(1, 0, 2),
        "b0t": a["L0_ffn_B"].transpose(0, 2, 1).reshape(ER0, O),
        "mixw": a["L1_cond_weights"],
        "w1": a["L1_ffn_W_base"].T,
        "b1": a["L1_ffn_b_base"][None, :],
        "a1": np.concatenate([a["L1_ffn_lora_A"].reshape(ETOT, R1, KC, P),
                              a["L1_ffn_router_W"].reshape(ETOT, 1, KC, P)], axis=1).transpose(0, 3, 2, 1),
        "b1t": a["L1_ffn_lora_B"].transpose(0, 2, 1),
        "rb": a["L1_ffn_router_b"],
        "prior": a["L1_ffn_domain_prior"],
    }
    nc = bacc.Bacc("TRN2", target_bir_lowering=False, num_devices=1, dynamic_dma_scratch_size=1024)
    arrays, d = {}, {}
    for name, v in laid.items():
        v = np.ascontiguousarray(v)
        arrays[f"in_{name}"] = v
        d[name] = nc.dram_tensor(f"in_{name}", v.shape, mybir.dt.from_np(v.dtype), kind="ExternalInput").ap()
    out = nc.dram_tensor("out", (NT, P, T), F32, kind="ExternalOutput").ap()
    build(nc, d, out)
    r = run_bass_kernel_spmd(nc, [arrays], core_ids=[0])
    return r.results[0]["out"].reshape(B, C, T)
```

```python
from contextlib import ExitStack

import numpy as np

import concourse.bass as bass
from concourse import mybir

F32 = mybir.dt.float32
F32R = mybir.dt.float32r
BF16 = mybir.dt.bfloat16
I32 = mybir.dt.int32
ALU = mybir.AluOpType
ACT = mybir.ActivationFunctionType
AX_X = mybir.AxisListType.X

P = 128
B, C, T = 128, 64, 1024
PAIR = P // C
NT = B // PAIR
O = T
KC = T // P
HALF = 512
KH = KC // 2
HID = 128
NS = 8
E0, R0 = 8, 16
ER0 = E0 * R0
X0 = ER0 + E0
NC = 16
ETOT, E1, R1 = 16, 4, 8
ER1 = E1 * R1
X1 = ER1 + E1
K1 = 3 * ER1 + 2
SCALING = 2.0
EPS = 1e-12
RING = 3
STAGES = 4

C_ID, C_RANK, C_T, C_CH, C_P, C_NLO = 0, P, P + E0, P + E0 + KC, P + E0 + KC + 1, P + E0 + KC + 2
C_ALL = C_NLO + 1


def constants():
    c = np.zeros((P, C_ALL), np.float32)
    p = np.arange(P)
    c[:, C_ID:C_ID + P] = np.eye(P)
    c[:, C_RANK:C_RANK + E0] = E0 - np.arange(E0)
    c[:, C_T:C_T + KC] = p[:, None] + P * np.arange(KC)
    c[:, C_CH] = p % C
    c[:, C_P] = p
    c[:, C_NLO] = -1.0 * ((p >= 2 * ER1) & (p != 3 * ER1))
    return c


class Step:

    def __init__(self, q, phase):
        self.q, self.phase = q, phase
        self.i = q * RING + phase

    def slot(self, d):
        return (self.phase + d) % RING

    def round(self, d):
        return self.q + (self.phase + d) // RING


def at_step(i):
    return Step(i // RING, i % RING)


def build(nc, d, out):
    ctx = ExitStack()
    with ctx:
        def sb(name, shape, dt=F32):
            return ctx.enter_context(nc.sbuf_tensor(name, shape, dt))

        def pb(name):
            return ctx.enter_context(nc.psum_tensor(name, [P, HALF], F32))

        def sem(name):
            return ctx.enter_context(nc.semaphore(name))

        def f32(ap):
            return ap.bitcast(F32)

        w0 = [sb(f"w0_{s}", [P, KC, O], F32R) for s in ("hi", "lo")]
        w1 = [sb(f"w1_{s}", [P, KC, O], F32R) for s in ("hi", "lo")]
        a0 = sb("a0", [P, KC, 2, X0], F32R)
        a1 = sb("a1", [P, KC, 2, X1], F32R)
        b0t = [sb(f"b0t_{s}", [ER0, O], F32R) for s in ("hi", "lo")]
        b1s = sb("b1_stack", [K1, O], F32R)
        w2x = [sb(f"w2x{b}", [HID, 2 * C], F32R) for b in range(PAIR)]
        w2z = [sb(f"w2z{b}", [HID, 2 * C], F32R) for b in range(PAIR)]
        const = sb("const", [P, C_ALL])
        ident = const[:, C_ID:C_ID + P]
        rank = const[:, C_RANK:C_RANK + E0]
        b2col = sb("b2_col", [P, 1])
        b0bc = sb("b0_bc", [P, O])
        sess_bias = sb("sess_bias", [HID, B])
        hbias = sb("hid_bias", [HID, PAIR])
        tmask = sb("tmask", [P, NT, KC * PAIR], BF16)
        cmask = sb("cmask", [P, B])
        ids = sb("ids", [1, 2 * B + E1], I32)
        prior = sb("prior", [P, E1])
        rbias = sb("rbias", [P, E1])
        logit_bias = sb("logit_bias", [P, E1])
        xr = sb("x_ring", [P, RING, T])
        xs = sb("xs", [P, 2, T], F32R)
        tmp = sb("tmp", [P, PAIR * HALF])
        part = sb("part", [P, HALF])
        cs = sb("cs", [P, T])
        g = [sb(f"g_{s}", [HID, PAIR, HALF], F32R) for s in ("hi", "lo")]
        with ExitStack() as setup:
            def early(name, shape, dt=F32):
                return setup.enter_context(nc.sbuf_tensor(name, shape, dt))

            w2raw = early("w2_raw", [HID, C])
            bsess = early("b_sess", [NS, HID])
            onehot = early("onehot", [NS, B])
            lens = early("lens", [P, B], I32)
            sess8 = early("sess8", [NS, B], I32)
            seqs = early("seqs", [P, B], I32)
            early("rest_of_c0", [P, 2 * T - C - HID - 4 * B])
            st2 = [early(f"stage{k}", [P, O]) for k in range(2)]
        c0 = [sb(f"c0_{s}", [P, KC, P], F32R) for s in ("hi", "lo")]
        c1 = [sb(f"c1_{s}", [P, KC, P], F32R) for s in ("hi", "lo")]
        wraw = sb("wsess_raw", [P, PAIR, HID])
        wd = sb("wd", [P, PAIR, HID], F32R)
        wl = sb("wl", [P, HID], F32R)
        vraw = sb("v_raw", [P, P])
        vs = sb("vs", [P, 2, P], F32R)
        ho0 = sb("ho0", [P, X0])
        ho1 = sb("ho1", [P, X1])
        lg = ho0[:, ER0:X0]
        top = sb("top", [P, 8])
        pick = [sb(f"pick{j}", [P, E0]) for j in range(2)]
        first = [sb(f"first{j}", [P, 1]) for j in range(2)]
        left = sb("left", [P, E0])
        gap = sb("gap", [P, 1])
        egap = sb("egap", [P, 1])
        ahead = sb("ahead", [P, 1])
        esum = sb("esum", [P, 1])
        wtop = [sb(f"wtop{j}", [P, 1]) for j in range(2)]
        wsel = [sb(f"wsel{j}", [P, E0]) for j in range(2)]
        wsum = sb("wsum", [P, E0])
        h0t = [sb(f"h0t_{s}", [ER0, P], F32R) for s in ("hi", "lo")]
        z1 = sb("z1", [P, E1])
        nmax = sb("nmax", [P, 1])
        ez = sb("ez", [P, E1])
        zsum = sb("zsum", [P, 1])
        zinv = sb("zinv", [P, 1])
        alpha = sb("alpha", [P, E1])
        hw1 = ho1[:, 0:X1].rearrange("p (e r) -> p e r", e=E1)[:, :, 0:R1]
        h1s = sb("h1_stack", [P, K1], F32R)
        h1t = sb("h1t", [K1, P], F32R)

        psM = [pb("psM0"), pb("psM1")]
        psC = [pb("psC0"), pb("psC1")]
        psH = [pb("psH0"), pb("psH1")]
        psR = [pb("psR0"), pb("psR1")]
        psV = [psH[0], psH[1], psC[0], psC[1]]

        setup_in = sem("setup_in")
        pick_in = sem("pick_in")
        stage_in = [sem(f"stage_in{s}") for s in range(STAGES)]
        stage_hi = sem("stage_hi")
        stage_lo = sem("stage_lo")
        v_zero = sem("v_zero")
        w2_zero = sem("w2_zero")
        w2_hi = sem("w2_hi")
        w2_split = sem("w2_split")
        tables = sem("tables")
        bias_ps = sem("bias_ps")
        logits_in = sem("logits_in")
        x_in = [[sem(f"x_in{s}{h}") for h in range(2)] for s in range(RING)]
        x_out = [[sem(f"x_out{s}{h}") for h in range(2)] for s in range(RING)]
        w_in = sem("w_in")
        v_in = sem("v_in")
        ws_hi = sem("ws_hi")
        w_split = sem("w_split")
        vs_hi = sem("vs_hi")
        v_split = sem("v_split")
        xhi_h = sem("xhi_h")
        xlo_h = sem("xlo_h")
        xb_h = sem("xb_h")
        hid_h = sem("hid_h")
        gelu_h = sem("gelu_h")
        ghi_h = sem("ghi_h")
        glo_h = sem("glo_h")
        co_h = sem("co_h")
        cm_h = sem("cm_h")
        c0hi_h = sem("c0hi_h")
        c0lo_h = sem("c0lo_h")
        a0_done = sem("a0_done")
        gap_done = sem("gap_done")
        egap_done = sem("egap_done")
        route0 = sem("route0")
        hw0_done = sem("hw0_done")
        t0_done = sem("t0_done")
        h0hi_done = sem("h0hi_done")
        h0lo_done = sem("h0lo_done")
        m0_h = sem("m0_h")
        x1_h = sem("x1_h")
        x1hi_h = sem("x1hi_h")
        x1lo_h = sem("x1lo_h")
        mix_b = sem("mix_b")
        vlo_b = sem("vlo_b")
        vsum_b = sem("vsum_b")
        part_h = sem("part_h")
        cs_h = sem("cs_h")
        turn_h = sem("turn_h")
        c1hi_h = sem("c1hi_h")
        c1lo_h = sem("c1lo_h")
        a1_done = sem("a1_done")
        nmax_done = sem("nmax_done")
        ez_done = sem("ez_done")
        route1 = sem("route1")
        hw1_done = sem("hw1_done")
        t1_done = sem("t1_done")
        h1t_done = sem("h1t_done")
        m1_h = sem("m1_h")
        x2_h = sem("x2_h")

        stages = [xr[:, 1, :], xr[:, 2, :], st2[0][:, :], st2[1][:, :]]

        def cols(ap):
            return ap.rearrange("p a n -> p (a n)")

        pieces = []
        for k in range(2):
            ks = slice(k * KH, k * KH + KH)
            pieces.append((cols(d["a0"][:, ks, :]), a0[:, ks, 0, :], a0[:, ks, 1, :]))
        for k in range(KC):
            pieces.append((d["w0"][k * P:(k + 1) * P, :], w0[0][:, k, :], w0[1][:, k, :]))
        pieces.append((d["b0t"], b0t[0][:, :], b0t[1][:, :]))
        for k in range(KC):
            pieces.append((d["w1"][k * P:(k + 1) * P, :], w1[0][:, k, :], w1[1][:, k, :]))
        GATHER_A, GATHER_B = len(pieces), len(pieces) + 1
        pieces.append((None, a1[:, :, 0, :], a1[:, :, 1, :]))
        pieces.append((None, None, None))
        SETUP_IN = 16 * 10
        STAGE_GATHERS = {GATHER_A: E1, GATHER_B: 3 * E1 + 2}

        def shaped(st, like):
            if len(like.shape) == 2:
                return st[:, 0:like.shape[1]]
            k, n = like.shape[1:]
            return st[:, 0:k * n].rearrange("p (k n) -> p k n", k=k)

        def staged(n):
            return sum(16 * STAGE_GATHERS.get(m, 1) for m in range(n % STAGES, n + 1, STAGES))

        block = ctx.enter_context(nc.Block())

        @block.sync
        def _(sp):
            def row(ap, n):
                return ap.partition_broadcast(n)

            def gather_w(s, dt):
                for b in range(PAIR):
                    n = sp.value_load(ids[0:1, bass.ds(s.i * PAIR + (PAIR * dt + b), 1)], min_val=0, max_val=NS - 1)
                    for r in range(2):
                        sp.dma_start(wraw[C * r:C * r + C, b, :],
                                     d["wsess"][bass.ds(n, 1), :, :].rearrange("a c n -> (a c) n")).then_inc(w_in, 16)

            def gather_v(s, dt):
                for b in range(PAIR):
                    n = sp.value_load(ids[0:1, bass.ds(s.i * PAIR + (B + PAIR * dt + b), 1)], min_val=0, max_val=NC - 1)
                    sp.dma_start(vraw[C * b:C * b + C, C * b:C * b + C],
                                 d["mixw"][bass.ds(n, 1), :, :].rearrange("a c n -> (a c) n")).then_inc(v_in, 16)

            def load(s, dt, h):
                hs = slice(HALF * h, HALF * h + HALF)
                sp.dma_start(xr[:, s.slot(dt), hs],
                             d["x"][bass.ds(s.i + dt, 1), :, hs].rearrange("a p n -> (a p) n")
                             ).then_inc(x_in[s.slot(dt)][h], 16)

            def store(s, dt, h):
                hs = slice(HALF * h, HALF * h + HALF)
                sp.dma_start(out[bass.ds(s.i + dt, 1), :, hs].rearrange("a p n -> (a p) n"),
                             xr[:, s.slot(dt), hs]).then_inc(x_out[s.slot(dt)][h], 16)

            def step(s, gw=True, gv=True, ld=True, st=True):
                if gw:
                    sp.wait_ge(w_split, s.i + 2)
                    gather_w(s, 2)
                if gv:
                    sp.wait_ge(v_split, s.i)
                    gather_v(s, 0)
                for h in range(2):
                    if st:
                        sp.wait_ge(x2_h, s.i * 2 + (h - 1))
                        store(s, -1, h)
                    if ld:
                        if st:
                            sp.wait_ge(x_out[s.slot(2)][h], (s.round(2)) * 16)
                        load(s, 2, h)

            sp.dma_start(ids[:, :], d["ids"]).then_inc(setup_in, 16)
            sp.dma_start(const[:, :], d["const"]).then_inc(setup_in, 16)
            sp.dma_start(w2raw[:, :], d["w2"]).then_inc(setup_in, 16)
            for b in range(PAIR):
                sp.dma_start(b2col[C * b:C * b + C, :], d["b2"]).then_inc(setup_in, 16)
            sp.dma_start(b0bc[:, :], row(d["b0"], P)).then_inc(setup_in, 16)
            sp.dma_start(bsess[:, :], d["bsess"]).then_inc(setup_in, 16)
            sp.dma_start(lens[:, :], row(d["lens"], P)).then_inc(setup_in, 16)
            sp.dma_start(sess8[:, :], row(d["sess"], NS)).then_inc(setup_in, 16)
            sp.dma_start(seqs[:, :], row(d["seqs"], P)).then_inc(setup_in, 16)
            for h in range(2):
                load(at_step(0), 0, h)
            sp.wait_ge(setup_in, SETUP_IN)
            active = [sp.value_load(ids[0:1, 2 * B + j:2 * B + j + 1], min_val=0, max_val=ETOT - 1)
                      for j in range(E1)]
            for j in range(E1):
                sp.dma_start(prior[:, j:j + 1], row(d["prior"][bass.ds(active[j], 1)], P)).then_inc(pick_in, 16)
                sp.dma_start(rbias[:, j:j + 1], row(d["rb"][bass.ds(active[j], 1)], P)).then_inc(pick_in, 16)
            sp.wait_ge(v_zero, 1)
            gather_w(at_step(0), 0)
            gather_v(at_step(0), 0)
            for n, (src, hi, _lo) in enumerate(pieces):
                st = stages[n % STAGES]
                if n >= STAGES:
                    sp.wait_ge(stage_lo, n - STAGES + 1)
                done = stage_in[n % STAGES]
                if src is not None:
                    sp.dma_start(st[:, 0:src.shape[1]], src).then_inc(done, 16)
                elif n == GATHER_A:
                    to = st[:, 0:KC * X1].rearrange("p (k n) -> p k n", k=KC)
                    for j in range(E1):
                        one = bass.ds(active[j], 1)
                        sp.dma_start(to[:, :, (R1 + 1) * j:(R1 + 1) * (j + 1)],
                                     d["a1"][one, :, :, :].rearrange("a p k r -> (a p) k r")).then_inc(done, 16)
                else:
                    for rep in range(3):
                        for j in range(E1):
                            r = rep * ER1 + R1 * j
                            sp.dma_start(st[r:r + R1, :], d["b1t"][bass.ds(active[j], 1), :, :]
                                         .rearrange("a r n -> (a r) n")).then_inc(done, 16)
                    for r in range(2):
                        sp.dma_start(st[3 * ER1 + r:3 * ER1 + r + 1, :], d["b1"]).then_inc(done, 16)
            sp.wait_ge(stage_lo, len(pieces))
            for h in range(2):
                load(at_step(0), 1, h)
            sp.wait_ge(w_split, 1)
            gather_w(at_step(0), 1)
            step(at_step(0), gv=False, st=False)
            with sp.Fori(0, (NT - 4) // RING) as q:
                for u in range(RING):
                    step(Step(q, 1 + u))
            step(at_step(NT - 3))
            step(at_step(NT - 2), gw=False, ld=False)
            step(at_step(NT - 1), gw=False, ld=False)
            step(at_step(NT), gw=False, gv=False, ld=False)
            for s in range(RING):
                for h in range(2):
                    sp.wait_ge(x_out[s][h], 16 * len(range(s, NT, RING)))

        @block.tensor
        def _(pe):
            def three(out_, left_, right_, start=True, stop=True):
                nc.tensor.matmul(out_, left_[0], right_[0], start=start, stop=False)
                nc.tensor.matmul(out_, left_[0], right_[1], start=False, stop=False)
                return nc.tensor.matmul(out_, left_[1], right_[0], start=False, stop=stop)

            def hidden(i, h):
                pe.wait_ge(xlo_h, i * 2 + (h + 1))
                if h == 0:
                    pe.wait_ge(w_split, i + 1)
                if h or not (isinstance(i, int) and i == 0):
                    pe.wait_ge(gelu_h, i * 2 + h)
                hs = slice(HALF * h, HALF * h + HALF)
                for bt in range(PAIR):
                    r = slice(C * bt, C * bt + C)
                    nc.tensor.matmul(psH[bt][:, :], wd[:, bt, :], xs[:, bt, hs], start=True, stop=False)
                    last = nc.tensor.matmul(psH[bt][:, :], wl[r, :], xs[r, bt, hs], start=False, stop=True)
                last.then_inc(hid_h, 1)

            def cond0(i, h):
                pe.wait_ge(glo_h, i * 2 + (h + 1))
                for bt in range(PAIR):
                    nc.tensor.matmul(psH[bt][:, :], w2x[bt][:, :], g[0][:, bt, :], start=True, stop=False)
                    last = nc.tensor.matmul(psH[bt][:, :], w2z[bt][:, :], g[1][:, bt, :], start=False, stop=True)
                last.then_inc(co_h, 1)

            def turn0(i, h, early=False):
                pe.wait_ge(cs_h, i * 2 + (h + 1))
                if not early:
                    pe.wait_ge(vsum_b, i * 4 - 4)
                for k in range(KH):
                    at = (KH * h + k) * P
                    last = nc.tensor.transpose(psC[h][:, k * P:(k + 1) * P], cs[:, at:at + P], ident)
                last.then_inc(turn_h, 1)

            def low(x, a, ps, n):
                for k in range(KC):
                    nc.tensor.matmul(ps[:, 0:2 * n], x[0][:, k, :], a[:, k, :, :].rearrange("p s n -> p (s n)"),
                                     start=(k == 0), stop=False)
                    last = nc.tensor.matmul(ps[:, 0:n], x[1][:, k, :], a[:, k, 0, :],
                                            start=False, stop=(k == KC - 1))
                return last

            def ffn(x, w, h, ks):
                for k in ks:
                    three(psM[h][:, :], [t[:, k, :] for t in x],
                          [t[:, k, HALF * h:HALF * h + HALF] for t in w], start=(k == 0), stop=False)

            def step(i, prep=True, l0=True, l1=True, early=False):
                if l0:
                    pe.wait_ge(c0lo_h, i * 2 + 2)
                    low(c0, a0, psR[0], X0).then_inc(a0_done, 1)
                    if l1 and not early:
                        pe.wait_ge(x2_h, i * 2 - 3)
                    ffn(c0, w0, 0, range(5))
                    if prep:
                        if l1:
                            pe.wait_ge(vsum_b, i * 4)
                        hidden(i + 1, 0)
                    ffn(c0, w0, 0, range(5, 7))
                    pe.wait_ge(hw0_done, i + 1)
                    nc.tensor.transpose(psR[0][:, 3 * P:4 * P], ho0[:, 0:ER0],
                                        ident).then_inc(t0_done, 1)
                    ffn(c0, w0, 0, range(7, KC))
                    if l1 and not early:
                        pe.wait_ge(x2_h, i * 2 - 2)
                    ffn(c0, w0, 1, range(1))
                    pe.wait_ge(h0lo_done, i + 1)
                    three(psM[0][:, :], [t[:, :] for t in h0t], [t[:, 0:HALF] for t in b0t],
                          start=False).then_inc(m0_h, 1)
                    ffn(c0, w0, 1, range(1, 4))
                    if prep:
                        cond0(i + 1, 0)
                    ffn(c0, w0, 1, range(4, KC))
                    if prep:
                        pe.wait_ge(cs_h, i * 2 + 3)
                        hidden(i + 1, 1)
                    three(psM[1][:, :], [t[:, :] for t in h0t], [t[:, HALF:O] for t in b0t],
                          start=False).then_inc(m0_h, 1)
                if l1:
                    pe.wait_ge(c1lo_h, i * 2)
                    low(c1, a1, psR[1], X1).then_inc(a1_done, 1)
                    if l0:
                        pe.wait_ge(x1_h, i * 2 + 1)
                    else:
                        pe.wait_ge(x2_h, i * 2 - 3)
                    ffn(c1, w1, 0, range(3))
                if l0 and prep:
                    cond0(i + 1, 1)
                if l1:
                    ffn(c1, w1, 0, range(3, 5))
                if l0 and prep:
                    turn0(i + 1, 0, early=not l1)
                if l1:
                    ffn(c1, w1, 0, range(5, 7))
                    pe.wait_ge(hw1_done, i)
                    nc.tensor.transpose(psR[1][0:K1, 2 * P:3 * P], f32(h1s[:, :]), ident).then_inc(t1_done, 1)
                    ffn(c1, w1, 0, range(7, KC))
                    if l0:
                        pe.wait_ge(x1_h, i * 2 + 2)
                    else:
                        pe.wait_ge(x2_h, i * 2 - 2)
                    ffn(c1, w1, 1, range(1))
                    pe.wait_ge(h1t_done, i)
                    nc.tensor.matmul(psM[0][:, :], h1t[:, :], b1s[:, 0:HALF],
                                     start=False, stop=True).then_inc(m1_h, 1)
                if l0 and prep:
                    turn0(i + 1, 1, early=not l1)
                if l1:
                    ffn(c1, w1, 1, range(1, KC))
                    nc.tensor.matmul(psM[1][:, :], h1t[:, :], b1s[:, HALF:O],
                                     start=False, stop=True).then_inc(m1_h, 1)
                if l0:
                    pe.wait_ge(v_split, i + 1)
                    pe.wait_ge(x1lo_h, i * 2 + 2)
                    if prep:
                        pe.wait_ge(cm_h, i * 2 + 4)
                    for k in range(KC):
                        ps = psV[k // 2][:, (k % 2) * 2 * P:(k % 2 + 1) * 2 * P]
                        nc.tensor.matmul(ps, xs[:, 0, k * P:(k + 1) * P],
                                         vs[:, :, :].rearrange("p s n -> p (s n)"), start=True, stop=False)
                        last = nc.tensor.matmul(ps[:, 0:P], xs[:, 1, k * P:(k + 1) * P], vs[:, 0, :],
                                                start=False, stop=True)
                        if k % 2:
                            last.then_inc(mix_b, 1)

            pe.wait_ge(tables, 1)
            pe.wait_ge(setup_in, SETUP_IN)
            nc.tensor.matmul(psR[0][:, 0:B], bsess[:, :], onehot[:, :], start=True, stop=True).then_inc(bias_ps, 1)
            pe.wait_ge(w2_split, 1)
            for h in range(2):
                if h:
                    pe.wait_ge(cs_h, 1)
                hidden(0, h)
                cond0(0, h)
                turn0(0, h, early=True)
            pe.wait_ge(stage_lo, len(pieces))
            step(0, l1=False)
            step(1, early=True)
            with pe.Fori(2, NT - 1) as i:
                step(i)
            step(NT - 1, prep=False)
            step(NT, prep=False, l0=False)

        @block.scalar
        def _(act):
            def hi(out_, in_):
                return nc.scalar.activation(out_, in_, ACT.Copy)

            def split_x(s, dt, h):
                hs = slice(HALF * h, HALF * h + HALF)
                act.wait_ge(x_in[s.slot(dt)][h], s.round(dt) * 16 + 16)
                for b in range(PAIR):
                    r = slice(C * b, C * b + C)
                    last = hi(xs[r, b, hs], xr[r, s.slot(dt), hs])
                last.then_inc(xhi_h, 1)

            def gelu(i, h, first=False):
                act.wait_ge(hid_h, i * 2 + (h + 1))
                if h:
                    act.wait_ge(glo_h, i * 2 + h)
                elif not first:
                    act.wait_ge(c1lo_h, i * 2 - 2)
                for bt in range(PAIR):
                    last = nc.scalar.activation(tmp[:, bt * HALF:(bt + 1) * HALF], psH[bt][:, :], ACT.Gelu,
                                                bias=hbias[:, bt:bt + 1])
                last.then_inc(gelu_h, 1)
                act.wait_ge(gelu_h, i * 2 + (h + 1))
                hi(g[0][:, :, :].rearrange("p b n -> p (b n)"), tmp[:, :]).then_inc(ghi_h, 1)

            def bias_c0(i, h, first=False):
                act.wait_ge(co_h, i * 2 + (h + 1))
                if not first:
                    act.wait_ge(cs_h, i * 2 + h)
                for b in range(PAIR):
                    r, q = slice(C * b, C * b + C), slice(C * (1 - b), C * (1 - b) + C)
                    last = nc.scalar.activation(part[r, :], psH[b][q, :], ACT.Identity, bias=b2col[q, 0:1])
                last.then_inc(part_h, 1)

            def split_c0(i, h):
                act.wait_ge(cm_h, i * 2 + (h + 1))
                hi(c0[0][:, KH * h:KH * h + KH, :].rearrange("p k n -> p (k n)"),
                   tmp[:, HALF * h:HALF * h + HALF]).then_inc(c0hi_h, 1)

            def step(s, prep=True, l0=True, l1=True, early=False):
                i = s.i
                if l1:
                    for v in range(4):
                        act.wait_ge(mix_b, i * 4 + (v - 3))
                        hi(cs[:, 2 * P * v:2 * P * v + 2 * P].rearrange("p (k n) -> p k n", k=2),
                           psV[v][:, :].rearrange("p (k s n) -> p k s n", k=2, s=2)[:, :, 1, :]).then_inc(vlo_b, 1)
                if prep:
                    split_x(s, 1, 0)
                if l0:
                    act.wait_ge(gap_done, i + 1)
                    nc.scalar.activation(egap[:, :], gap[:, :], ACT.Exp).then_inc(egap_done, 1)
                if prep:
                    nc.scalar.activation(ahead[:, :], const[:, C_P:C_P + 1], ACT.Gelu)
                if l1:
                    if not early:
                        act.wait_ge(m1_h, i * 2 - 2)
                    for h in range(2):
                        act.wait_ge(vsum_b, i * 4 + (2 * h - 2))
                        hi(c1[0][:, KH * h:KH * h + KH, :].rearrange("p k n -> p (k n)"),
                           tmp[:, HALF * h:HALF * h + HALF]).then_inc(c1hi_h, 1)
                if prep:
                    split_x(s, 1, 1)
                if l0:
                    act.wait_ge(t0_done, i + 1)
                    hi(h0t[0][:, :], psR[0][:, 3 * P:4 * P]).then_inc(h0hi_done, 1)
                if prep:
                    gelu(i + 1, 0, first=not l1)
                    bias_c0(i + 1, 0)
                    gelu(i + 1, 1)
                    nc.scalar.activation(ahead[:, :], const[:, C_CH:C_CH + 1], ACT.Exp)
                if l1:
                    act.wait_ge(nmax_done, i)
                    nc.scalar.activation(ez[:, :], z1[:, :], ACT.Exp, bias=nmax[:, 0:1],
                                         accum_out=zsum[:, :]).then_inc(ez_done, 1)
                if l0:
                    for h in range(2):
                        hs = slice(HALF * h, HALF * h + HALF)
                        act.wait_ge(x1_h, i * 2 + (h + 1))
                        hi(xs[:, 0, hs], xr[:, s.slot(0), hs]).then_inc(x1hi_h, 1)
                if prep:
                    bias_c0(i + 1, 1)
                if l1:
                    act.wait_ge(t1_done, i)
                    hi(h1t[:, :], psR[1][0:K1, 2 * P:3 * P]).then_inc(h1t_done, 1)
                if prep:
                    act.wait_ge(m0_h, i * 2 + 2)
                    for h in range(2):
                        split_c0(i + 1, h)

            act.wait_ge(tables, 2)
            nc.scalar.activation(prior[:, :], prior[:, :], ACT.Ln).then_inc(logits_in, 1)
            act.wait_ge(setup_in, SETUP_IN)
            act.wait_ge(w2_zero, 1)
            for b in range(PAIR):
                hi(w2z[b][:, C * b:C * b + C], w2raw[:, :])
                last = hi(w2x[b][:, C * b:C * b + C], w2raw[:, :])
            last.then_inc(w2_hi, 1)

            def piece(n):
                _src, hi_, _lo = pieces[n]
                st = stages[n % STAGES]
                act.wait_ge(stage_in[n % STAGES], staged(n))
                if n == GATHER_B:
                    hi(b1s[:, :], st[0:K1, :]).then_inc(stage_hi, 1)
                else:
                    hi(hi_, shaped(st, hi_)).then_inc(stage_hi, 1)

            between = {2: lambda: (split_x(at_step(0), 0, 0), split_x(at_step(0), 0, 1)),
                       5: lambda: gelu(0, 0, first=True), 8: lambda: bias_c0(0, 0, first=True),
                       11: lambda: gelu(0, 1), 14: lambda: bias_c0(0, 1)}
            for n in range(len(pieces)):
                piece(n)
                if n in between:
                    between[n]()
            for h in range(2):
                split_c0(0, h)
            step(at_step(0), l1=False)
            step(at_step(1), early=True)
            step(at_step(2))
            step(at_step(3))
            with act.Fori(1, NT // RING - 1) as q:
                for u in range(RING):
                    step(Step(q, 1 + u))
            for i in range(RING * (NT // RING - 1) + 1, NT - 1):
                step(at_step(i))
            step(at_step(NT - 1), prep=False)
            step(at_step(NT), prep=False, l0=False)

        @block.vector
        def _(dve):
            tt, ts, stt = nc.vector.tensor_tensor, nc.vector.tensor_scalar, nc.vector.scalar_tensor_tensor

            def lo(out_, in_, hi_):
                return tt(out_, in_, f32(hi_), ALU.subtract)

            def split_w(i, first=False):
                dve.wait_ge(w_in, i * (32 * PAIR) + 32 * PAIR)
                if not first:
                    dve.wait_ge(hid_h, i * 2)
                ts(hbias[:, :], sess_bias[:, bass.ds(i * PAIR, PAIR)], 1.0, None, ALU.mult)
                for b in range(PAIR):
                    last = ts(wd[:, b, :], wraw[:, b, :], cmask[:, bass.ds(i * PAIR + b, 1)], None, ALU.mult)
                last.then_inc(ws_hi, 1)
                dve.wait_ge(ws_hi, i + 1)
                for b in range(PAIR):
                    r = slice(C * b, C * b + C)
                    last = stt(wl[r, :], wraw[r, b, :], cmask[r, bass.ds(i * PAIR + b, 1)], f32(wd[r, b, :]),
                               ALU.mult, ALU.subtract)
                last.then_inc(w_split, 1)

            def split_v(i):
                dve.wait_ge(v_in, i * (16 * PAIR) + 16 * PAIR)
                nc.vector.tensor_copy(vs[:, 0, :], vraw[:, :]).then_inc(vs_hi, 1)
                dve.wait_ge(vs_hi, i + 1)
                lo(vs[:, 1, :], vraw[:, :], vs[:, 0, :]).then_inc(v_split, 1)

            def split_x(s, dt, h):
                hs = slice(HALF * h, HALF * h + HALF)
                dve.wait_ge(xhi_h, s.i * 2 + (2 * dt + h + 1))
                for b in range(PAIR):
                    r, q = slice(C * b, C * b + C), slice(C * (1 - b), C * (1 - b) + C)
                    last = lo(xs[q, b, hs], xr[r, s.slot(dt), hs], xs[r, b, hs])
                last.then_inc(xlo_h, 1)

            def split_g(i, h):
                dve.wait_ge(ghi_h, i * 2 + (h + 1))
                lo(g[1][:, :, :].rearrange("p b n -> p (b n)"), tmp[:, :],
                   g[0][:, :, :].rearrange("p b n -> p (b n)")).then_inc(glo_h, 1)

            def sum_c0(i, h):
                dve.wait_ge(part_h, i * 2 + (h + 1))
                hs = slice(HALF * h, HALF * h + HALF)
                for b in range(PAIR):
                    r = slice(C * b, C * b + C)
                    last = tt(cs[r, hs], psH[b][r, :], part[r, :], ALU.add)
                last.then_inc(cs_h, 1)

            def mask_c0(i, h):
                dve.wait_ge(turn_h, i * 2 + (h + 1))
                dve.wait_ge(glo_h, i * 2 + 2)
                m = tmask[:, bass.ds(i, 1), h * (HALF // C):(h + 1) * (HALF // C)].rearrange("p a m -> p (a m)")
                tt(tmp[:, HALF * h:HALF * h + HALF].rearrange("p (m s) -> p m s", s=C),
                   psC[h][:, :].rearrange("p (m s) -> p m s", s=C),
                   m.unsqueeze(2).to_broadcast([P, HALF // C, C]), ALU.mult).then_inc(cm_h, 1)

            def split_c0(i, h):
                dve.wait_ge(c0hi_h, i * 2 + (h + 1))
                t = slice(KH * h, KH * h + KH)
                lo(c0[1][:, t, :].rearrange("p k n -> p (k n)"), tmp[:, HALF * h:HALF * h + HALF],
                   c0[0][:, t, :].rearrange("p k n -> p (k n)")).then_inc(c0lo_h, 1)

            ROUTE0, ROUTE1 = 15, 7

            def route_0(i):
                done = [0]

                def link(ins, sync=True):
                    done[0] += 1
                    ins.then_inc(route0, 1)
                    if sync:
                        dve.wait_ge(route0, i * ROUTE0 + done[0])

                dve.wait_ge(a0_done, i + 1)
                link(nc.vector.tensor_copy(ho0[:, :], psR[0][:, X0:2 * X0]))
                link(tt(lg, lg, psR[0][:, ER0:X0], ALU.add))
                link(tt(ho0[:, 0:ER0], ho0[:, 0:ER0], psR[0][:, 0:ER0], ALU.add), sync=False)
                link(nc.vector.max(top[:, :], lg))
                tt(gap[:, :], top[:, 1:2], top[:, 0:1], ALU.subtract).then_inc(gap_done, 1)
                link(stt(pick[0][:, :], lg, top[:, 0:1], rank, ALU.is_equal, ALU.mult))
                link(nc.vector.tensor_reduce(first[0][:, :], pick[0][:, :], AX_X, ALU.max))
                link(stt(left[:, :], rank, first[0][:, 0:1], rank, ALU.not_equal, ALU.mult))
                link(stt(pick[1][:, :], lg, top[:, 1:2], left[:, :], ALU.is_equal, ALU.mult))
                link(nc.vector.tensor_reduce(first[1][:, :], pick[1][:, :], AX_X, ALU.max), sync=False)
                dve.wait_ge(egap_done, i + 1)
                link(ts(esum[:, :], egap[:, :], 1.0, 1.0 / SCALING, ALU.add, ALU.mult))
                link(nc.vector.reciprocal(wtop[0][:, :], esum[:, :]))
                link(ts(wtop[1][:, :], egap[:, :], wtop[0][:, 0:1], None, ALU.mult), sync=False)
                link(ts(wsel[0][:, :], rank, first[0][:, 0:1], wtop[0][:, 0:1], ALU.is_equal, ALU.mult))
                link(ts(wsel[1][:, :], rank, first[1][:, 0:1], wtop[1][:, 0:1], ALU.is_equal, ALU.mult))
                link(tt(wsum[:, :], wsel[0][:, :], wsel[1][:, :], ALU.add))
                assert done[0] == ROUTE0
                low = ho0[:, 0:ER0].rearrange("p (e r) -> p e r", e=E0)
                tt(low, low,
                   wsum[:, :].unsqueeze(2).to_broadcast([P, E0, R0]), ALU.mult).then_inc(hw0_done, 1)

            def link_1(i, n, ins):
                ins.then_inc(route1, 1)
                dve.wait_ge(route1, i * ROUTE1 + n)

            def logits_1(i):
                dve.wait_ge(a1_done, i + 1)
                link_1(i, 1, nc.vector.tensor_copy(ho1[:, :], psR[1][:, X1:2 * X1]))
                link_1(i, 2, tt(ho1[:, :], ho1[:, :], psR[1][:, 0:X1], ALU.add))
                out1 = ho1[:, :].rearrange("p (e r) -> p e r", e=E1)
                link_1(i, 3, tt(z1[:, :], out1[:, :, R1:R1 + 1].rearrange("p e r -> p (e r)"),
                                logit_bias[:, :], ALU.add))
                nc.vector.tensor_reduce(nmax[:, :], z1[:, :], AX_X, ALU.max, negate=True).then_inc(nmax_done, 1)

            def route_1(i):
                dve.wait_ge(ez_done, i + 1)
                link_1(i, 4, nc.vector.reciprocal(zinv[:, :], zsum[:, :]))
                link_1(i, 5, ts(alpha[:, :], ez[:, :], zinv[:, 0:1], SCALING, ALU.mult, ALU.mult))
                link_1(i, 6, tt(hw1, hw1, alpha[:, :].unsqueeze(2).to_broadcast([P, E1, R1]), ALU.mult))
                stack = h1s[:, 0:3 * ER1].rearrange("p (s e r) -> p s e r", s=3, e=E1)
                link_1(i, ROUTE1, nc.vector.tensor_copy(stack[:, 0], hw1))
                nc.vector.tensor_copy(stack[:, 2], hw1)
                lo(stack[:, 1], hw1, stack[:, 0]).then_inc(hw1_done, 1)

            def split_c1(i, h):
                t = slice(KH * h, KH * h + KH)
                dve.wait_ge(c1hi_h, i * 2 + (h + 1))
                lo(c1[1][:, t, :].rearrange("p k n -> p (k n)"), tmp[:, HALF * h:HALF * h + HALF],
                   c1[0][:, t, :].rearrange("p k n -> p (k n)")).then_inc(c1lo_h, 1)

            def step(s, prep=True, l0=True, l1=True, more=True):
                i = s.i

                def add_x1(h):
                    hs = slice(HALF * h, HALF * h + HALF)
                    dve.wait_ge(m0_h, i * 2 + (h + 1))
                    dve.wait_ge(xb_h, i * 2 + (h + 1))
                    tt(xr[:, s.slot(0), hs], xr[:, s.slot(0), hs], psM[h][:, :], ALU.add).then_inc(x1_h, 1)

                def add_x2(h):
                    hs = slice(HALF * h, HALF * h + HALF)
                    dve.wait_ge(m1_h, i * 2 + (h - 1))
                    tt(xr[:, s.slot(-1), hs], xr[:, s.slot(-1), hs], psM[h][:, :], ALU.add).then_inc(x2_h, 1)

                if l1:
                    if l0:
                        dve.wait_ge(c0lo_h, i * 2 + 2)
                    else:
                        dve.wait_ge(c1lo_h, i * 2 - 2)
                    for v in range(4):
                        dve.wait_ge(vlo_b, i * 4 + (v - 3))
                        tt(tmp[:, 2 * P * v:2 * P * v + 2 * P].rearrange("p (k n) -> p k n", k=2),
                           psV[v][:, :].rearrange("p (k s n) -> p k s n", k=2, s=2)[:, :, 0, :],
                           cs[:, 2 * P * v:2 * P * v + 2 * P].rearrange("p (k n) -> p k n", k=2),
                           ALU.add).then_inc(vsum_b, 1)
                if prep:
                    split_x(s, 1, 0)
                if l0:
                    route_0(i)
                if l1:
                    split_c1(i - 1, 0)
                if l0:
                    dve.wait_ge(h0hi_done, i + 1)
                    lo(h0t[1][:, :], psR[0][:, 3 * P:4 * P], h0t[0][:, :]).then_inc(h0lo_done, 1)
                if l1:
                    split_c1(i - 1, 1)
                if prep:
                    split_x(s, 1, 1)
                    split_g(i + 1, 0)
                if l0:
                    add_x1(0)
                if prep:
                    sum_c0(i + 1, 0)
                if l0:
                    add_x1(1)
                if l1:
                    logits_1(i - 1)
                if prep:
                    split_g(i + 1, 1)
                if l1:
                    route_1(i - 1)
                if l0:
                    for h in range(2):
                        hs = slice(HALF * h, HALF * h + HALF)
                        dve.wait_ge(x1hi_h, i * 2 + (h + 1))
                        lo(xs[:, 1, hs], xr[:, s.slot(0), hs], xs[:, 0, hs]).then_inc(x1lo_h, 1)
                if prep:
                    sum_c0(i + 1, 1)
                if l0:
                    split_v(i)
                if prep:
                    mask_c0(i + 1, 0)
                    split_c0(i + 1, 0)
                if l1:
                    add_x2(0)
                if prep:
                    mask_c0(i + 1, 1)
                    split_c0(i + 1, 1)
                    if more:
                        split_w(i + 2)
                if l1:
                    add_x2(1)

            nc.vector.memset(vraw[:, :], 0.0).then_inc(v_zero, 1)
            for b in range(PAIR):
                last = nc.vector.memset(f32(w2z[b][:, :]), 0.0)
            last.then_inc(w2_zero, 1)
            dve.wait_ge(setup_in, SETUP_IN)
            ts(onehot[:, :], sess8[:, :], const[0:NS, C_P:C_P + 1], None, ALU.is_equal).then_inc(tables, 1)
            dve.wait_ge(pick_in, 16 * 2 * E1)
            ts(prior[:, :], prior[:, :], EPS, None, ALU.add).then_inc(tables, 1)
            ts(cmask[:, :], lens[:, :], const[:, C_CH:C_CH + 1], None, ALU.is_gt)
            m = tmask[:, :, :].rearrange("p n (k b) -> p n k b", b=PAIR)
            for k in range(KC):
                last = ts(m[:, :, k, :], seqs[:, :].rearrange("p (n b) -> p n b", b=PAIR),
                          const[:, C_T + k:C_T + k + 1], None, ALU.is_gt)
            nc.vector.memset(f32(h1s[:, 3 * ER1:K1]), 1.0)
            last.then_inc(tables, 1)
            dve.wait_ge(tables, 3)
            dve.wait_ge(bias_ps, 1)
            nc.vector.tensor_copy(sess_bias[:, :], psR[0][:, 0:B]).then_inc(tables, 1)
            dve.wait_ge(logits_in, 1)
            tt(logit_bias[:, :], prior[:, :], rbias[:, :], ALU.add)
            dve.wait_ge(w2_hi, 1)
            for b in range(PAIR):
                last = lo(w2x[b][:, C * (1 - b):C * (1 - b) + C], w2raw[:, :], w2x[b][:, C * b:C * b + C])
            last.then_inc(w2_split, 1)
            dve.wait_ge(tables, 4)
            split_w(0, first=True)

            def piece(n):
                _src, _hi, lo_ = pieces[n]
                dve.wait_ge(stage_hi, n + 1)
                st = stages[n % STAGES]
                if n == GATHER_B:
                    r = slice(2 * ER1, K1)
                    stt(b1s[r, :], f32(b1s[r, :]), const[r, C_NLO:C_NLO + 1], st[r, :],
                        ALU.mult, ALU.add).then_inc(stage_lo, 1)
                else:
                    lo(lo_, shaped(st, lo_), _hi).then_inc(stage_lo, 1)

            between = {2: lambda: (split_x(at_step(0), 0, 0), split_x(at_step(0), 0, 1)),
                       5: lambda: split_g(0, 0), 8: lambda: sum_c0(0, 0),
                       11: lambda: split_g(0, 1), 14: lambda: sum_c0(0, 1)}
            for n in range(len(pieces)):
                piece(n)
                if n in between:
                    between[n]()
            for h in range(2):
                mask_c0(0, h)
                split_c0(0, h)
            split_w(1)
            step(at_step(0), l1=False)
            with dve.Fori(0, NT // RING - 1) as q:
                for u in range(RING):
                    step(Step(q, 1 + u))
            for i in range(RING * (NT // RING - 1) + 1, NT - 1):
                step(at_step(i), more=i + 2 < NT)
            step(at_step(NT - 1), prep=False)
            step(at_step(NT), prep=False, l0=False)

        @block.gpsimd
        def _(pool):
            def bias_x(s, dt, h):
                hs = slice(HALF * h, HALF * h + HALF)
                pool.wait_ge(xlo_h, s.i * 2 + (2 * dt + h + 1))
                nc.gpsimd.tensor_tensor(xr[:, s.slot(dt), hs], xr[:, s.slot(dt), hs], b0bc[:, hs],
                                        ALU.add).then_inc(xb_h, 1)

            pool.wait_ge(setup_in, SETUP_IN)
            for h in range(2):
                bias_x(at_step(0), 0, h)
            for h in range(2):
                bias_x(at_step(0), 1, h)
            with pool.Fori(0, NT // RING - 1) as q:
                for u in range(RING):
                    for h in range(2):
                        bias_x(Step(q, 1 + u), 1, h)
            for i in range(RING * (NT // RING - 1) + 1, NT - 1):
                for h in range(2):
                    bias_x(at_step(i), 1, h)


def kernel(**inputs):
    import concourse.bacc as bacc
    from concourse.bass_utils import run_bass_kernel_spmd

    a = {k: np.ascontiguousarray(v) for k, v in inputs.items()}
    sess, seqs, cond, lens = a["itok_B_0_7"], a["itok_B_2182_4065"], a["itok_B_0_15"], a["_lenS"]
    laid = {
        "x": a["x"].reshape(NT, P, T),
        "ids": np.concatenate([sess, cond, a["L1_ffn_active"]])[None, :],
        "lens": lens,
        "sess": sess,
        "seqs": seqs,
        "const": constants(),
        "wsess": a["L0_cond_W_sess"],
        "bsess": a["L0_cond_b_sess"],
        "w2": a["L0_cond_W2"],
        "b2": a["L0_cond_b2"][:, None],
        "w0": a["L0_ffn_W_base"].T,
        "b0": a["L0_ffn_b_base"],
        "a0": np.concatenate([a["L0_ffn_A"].reshape(ER0, T), a["L0_ffn_W_router"]]).T
              .reshape(KC, P, X0).transpose(1, 0, 2),
        "b0t": a["L0_ffn_B"].transpose(0, 2, 1).reshape(ER0, O),
        "mixw": a["L1_cond_weights"],
        "w1": a["L1_ffn_W_base"].T,
        "b1": a["L1_ffn_b_base"][None, :],
        "a1": np.concatenate([a["L1_ffn_lora_A"].reshape(ETOT, R1, KC, P),
                              a["L1_ffn_router_W"].reshape(ETOT, 1, KC, P)], axis=1).transpose(0, 3, 2, 1),
        "b1t": a["L1_ffn_lora_B"].transpose(0, 2, 1),
        "rb": a["L1_ffn_router_b"],
        "prior": a["L1_ffn_domain_prior"],
    }
    nc = bacc.Bacc("TRN2", target_bir_lowering=False, num_devices=1, dynamic_dma_scratch_size=1024)
    arrays, d = {}, {}
    for name, v in laid.items():
        v = np.ascontiguousarray(v)
        arrays[f"in_{name}"] = v
        d[name] = nc.dram_tensor(f"in_{name}", v.shape, mybir.dt.from_np(v.dtype), kind="ExternalInput").ap()
    out = nc.dram_tensor("out", (NT, P, T), F32, kind="ExternalOutput").ap()
    build(nc, d, out)
    r = run_bass_kernel_spmd(nc, [arrays], core_ids=[0])
    return r.results[0]["out"].reshape(B, C, T)
```

```python
from contextlib import ExitStack

import numpy as np

import concourse.bass as bass
from concourse import mybir

F32 = mybir.dt.float32
F32R = mybir.dt.float32r
BF16 = mybir.dt.bfloat16
I32 = mybir.dt.int32
ALU = mybir.AluOpType
ACT = mybir.ActivationFunctionType
AX_X = mybir.AxisListType.X

P = 128
B, C, T = 128, 64, 1024
PAIR = P // C
NT = B // PAIR
O = T
KC = T // P
HALF = 512
KH = KC // 2
HID = 128
NS = 8
E0, R0 = 8, 16
ER0 = E0 * R0
X0 = ER0 + E0
NC = 16
ETOT, E1, R1 = 16, 4, 8
ER1 = E1 * R1
X1 = ER1 + E1
S0, S1 = 388, 352
MID0, MID1 = O - 2 * S0, O - 2 * S1
N0, N1 = X0 + O, X1 + O
W0_PIECES = 10
K1 = 3 * ER1 + 2
SCALING = 2.0
EPS = 1e-12
RING = 3
STAGES = 4

C_ID, C_RANK, C_T, C_CH, C_P, C_NLO = 0, P, P + E0, P + E0 + KC, P + E0 + KC + 1, P + E0 + KC + 2
C_ALL = C_NLO + 1


def constants():
    c = np.zeros((P, C_ALL), np.float32)
    p = np.arange(P)
    c[:, C_ID:C_ID + P] = np.eye(P)
    c[:, C_RANK:C_RANK + E0] = E0 - np.arange(E0)
    c[:, C_T:C_T + KC] = p[:, None] + P * np.arange(KC)
    c[:, C_CH] = p % C
    c[:, C_P] = p
    c[:, C_NLO] = -1.0 * (((p < 3 * ER1) & (p // R1 % 3 == 2)) | (p == K1 - 1))
    return c


class Step:

    def __init__(self, q, phase):
        self.q, self.phase = q, phase
        self.i = q * RING + phase

    def slot(self, d):
        return (self.phase + d) % RING

    def round(self, d):
        return self.q + (self.phase + d) // RING


def at_step(i):
    return Step(i // RING, i % RING)


def build(nc, d, out):
    ctx = ExitStack()
    with ctx:
        def sb(name, shape, dt=F32):
            return ctx.enter_context(nc.sbuf_tensor(name, shape, dt))

        def pb(name):
            return ctx.enter_context(nc.psum_tensor(name, [P, HALF], F32))

        def sem(name):
            return ctx.enter_context(nc.semaphore(name))

        def f32(ap):
            return ap.bitcast(F32)

        w0 = [sb(f"w0_{s}", [P, KC * N0], F32R) for s in ("hi", "lo")]
        w1 = [sb(f"w1_{s}", [P, KC, N1], F32R) for s in ("hi", "lo")]
        b0t = [sb(f"b0t_{s}", [ER0, O], F32R) for s in ("hi", "lo")]
        b1s = sb("b1_stack", [K1, O], F32R)
        w2x = [sb(f"w2x{b}", [HID, 2 * C], F32R) for b in range(PAIR)]
        w2z = [sb(f"w2z{b}", [HID, 2 * C], F32R) for b in range(PAIR)]
        const = sb("const", [P, C_ALL])
        ident = const[:, C_ID:C_ID + P]
        rank = const[:, C_RANK:C_RANK + E0]
        b2col = sb("b2_col", [P, 1])
        b0bc = sb("b0_bc", [P, O])
        sess_bias = sb("sess_bias", [HID, B])
        hbias = sb("hid_bias", [HID, PAIR])
        tmask = sb("tmask", [P, NT, KC * PAIR], BF16)
        cmask = sb("cmask", [P, B])
        ids = sb("ids", [1, 2 * B + E1], I32)
        picked = sb("picked", [P, E1, 2])
        prior, rbias = picked[:, :, 0], picked[:, :, 1]
        logit_bias = sb("logit_bias", [P, E1])
        xr = sb("x_ring", [P, RING, T])
        xs = sb("xs", [P, 2, T], F32R)
        tmp = sb("tmp", [P, PAIR * HALF])
        xa = sb("x_ahead", [P, HALF])
        cs = sb("cs", [P, T])
        g = [sb(f"g_{s}", [HID, PAIR, HALF], F32R) for s in ("hi", "lo")]
        with ExitStack() as setup:
            def early(name, shape, dt=F32):
                return setup.enter_context(nc.sbuf_tensor(name, shape, dt))

            w2raw = early("w2_raw", [HID, C])
            bsess = early("b_sess", [NS, HID])
            onehot = early("onehot", [NS, B])
            per_batch = early("per_batch", [P, 3, B], I32)
            sess8, lens, seqs = per_batch[0:NS, 0, :], per_batch[:, 1, :], per_batch[:, 2, :]
            early("rest_of_c0", [P, 2 * T - C - HID - 4 * B])
            st2 = [early(f"stage{k}", [P, O]) for k in range(2)]
        c0 = [sb(f"c0_{s}", [P, KC, P], F32R) for s in ("hi", "lo")]
        c1 = [sb(f"c1_{s}", [P, KC, P], F32R) for s in ("hi", "lo")]
        wraw = sb("wsess_raw", [P, PAIR, HID])
        wd = sb("wd", [P, PAIR, HID], F32R)
        wl = sb("wl", [P, HID], F32R)
        vraw = sb("v_raw", [P, P])
        vs = sb("vs", [P, 2, P], F32R)
        ho0 = sb("ho0", [P, ER0])
        ho1 = sb("ho1", [P, ER1])
        lg = sb("logits0", [P, E0])
        top = sb("top", [P, 8])
        pick = [sb(f"pick{j}", [P, E0]) for j in range(2)]
        first = [sb(f"first{j}", [P, 1]) for j in range(2)]
        left = sb("left", [P, E0])
        gap = sb("gap", [P, 1])
        egap = sb("egap", [P, 1])
        ahead = sb("ahead", [P, 1])
        esum = sb("esum", [P, 1])
        wtop = [sb(f"wtop{j}", [P, 1]) for j in range(2)]
        wsel = [sb(f"wsel{j}", [P, E0]) for j in range(2)]
        wsum = sb("wsum", [P, E0])
        h0t = [sb(f"h0t_{s}", [ER0, P], F32R) for s in ("hi", "lo")]
        z1 = sb("z1", [P, E1])
        nmax = sb("nmax", [P, 1])
        ez = sb("ez", [P, E1])
        zsum = sb("zsum", [P, 1])
        zinv = sb("zinv", [P, 1])
        alpha = sb("alpha", [P, E1])
        hw1 = ho1[:, :].rearrange("p (e r) -> p e r", e=E1)
        h1s = sb("h1_stack", [P, K1], F32R)
        h1t = sb("h1t", [K1, P], F32R)

        psM = [pb("psM0"), pb("psM1")]
        psC = [pb("psC0"), pb("psC1")]
        psH = [pb("psH0"), pb("psH1")]
        psR = [pb("psR0"), pb("psR1")]
        psB = [psC[1], psR[0]]
        turned = [psR[0][:, 3 * P:4 * P], psR[1][0:K1, 3 * P:4 * P]]
        psV = [psH[0], psH[1], psC[0], psC[1]]

        ids_in = sem("ids_in")
        setup_in = sem("setup_in")
        b0_in = sem("b0_in")
        pick_in = sem("pick_in")
        stage_in = [sem(f"stage_in{s}") for s in range(STAGES)]
        stage_hi = sem("stage_hi")
        stage_lo = sem("stage_lo")
        v_zero = sem("v_zero")
        w2_zero = sem("w2_zero")
        w2_hi = sem("w2_hi")
        w2_split = sem("w2_split")
        tables = sem("tables")
        tmask_done = sem("tmask_done")
        logit_bias_done = sem("logit_bias_done")
        bias_ps = sem("bias_ps")
        logits_in = sem("logits_in")
        xa_in = sem("xa_in")
        x_in = [sem(f"x_in{s}") for s in range(RING)]
        x_out = [[sem(f"x_out{s}{h}") for h in range(2)] for s in range(RING)]
        w_in = sem("w_in")
        v_in = sem("v_in")
        ws_hi = sem("ws_hi")
        w_split = sem("w_split")
        vs_hi = sem("vs_hi")
        v_split = sem("v_split")
        xhi_h = sem("xhi_h")
        xlo_h = sem("xlo_h")
        xb_h = sem("xb_h")
        hid_h = sem("hid_h")
        gelu_h = sem("gelu_h")
        ghi_h = sem("ghi_h")
        glo_h = sem("glo_h")
        co_h = sem("co_h")
        cm_h = sem("cm_h")
        c0hi_h = sem("c0hi_h")
        c0lo_h = sem("c0lo_h")
        a0_done = sem("a0_done")
        gap_done = sem("gap_done")
        egap_done = sem("egap_done")
        route0 = sem("route0")
        hw0_done = sem("hw0_done")
        t0_done = sem("t0_done")
        h0hi_done = sem("h0hi_done")
        h0lo_done = sem("h0lo_done")
        m0_h = sem("m0_h")
        x1_h = sem("x1_h")
        x1hi_h = sem("x1hi_h")
        x1lo_h = sem("x1lo_h")
        mix_b = sem("mix_b")
        vlo_b = sem("vlo_b")
        vsum_b = sem("vsum_b")
        part_h = sem("part_h")
        cs_h = sem("cs_h")
        turn_h = sem("turn_h")
        c1hi_h = sem("c1hi_h")
        c1lo_h = sem("c1lo_h")
        a1_done = sem("a1_done")
        nmax_done = sem("nmax_done")
        ez_done = sem("ez_done")
        route1 = sem("route1")
        hw1_done = sem("hw1_done")
        t1_done = sem("t1_done")
        h1t_done = sem("h1t_done")
        m1_h = sem("m1_h")
        mid0 = sem("mid0")
        mid1 = sem("mid1")
        x2_h = sem("x2_h")

        stages = [xr[:, 1, :], xr[:, 2, :], st2[0][:, :], st2[1][:, :]]

        pieces = []
        for k in range(W0_PIECES):
            n = slice(k * KC * N0 // W0_PIECES, (k + 1) * KC * N0 // W0_PIECES)
            pieces.append((d["w0"][:, n], w0[0][:, n], w0[1][:, n]))
        pieces.append((d["b0t"], b0t[0][:, :], b0t[1][:, :]))
        L0_PIECES = len(pieces)
        for k in range(KC):
            pieces.append((d["w1"][k * P:(k + 1) * P, :], w1[0][:, k, X1:N1], w1[1][:, k, X1:N1]))
        GATHER_A, GATHER_B = len(pieces), len(pieces) + 1
        pieces.append((None, w1[0][:, :, 0:X1], w1[1][:, :, 0:X1]))
        pieces.append((None, None, None))
        SETUP_IN = 16 * 6
        STAGE_GATHERS = {GATHER_A: E1, GATHER_B: E1 + 1}
        buffer = [n % STAGES for n in range(L0_PIECES)] + [1, 2, 3, 1, 2, 3, 2, 3, 2, 3]
        assert len(buffer) == len(pieces)

        def last_in(slot_buffer, n):
            return max((m for m in range(n) if buffer[m] == slot_buffer), default=None)

        SPARE = (range(0, 3), range(3, 6), range(6, 8), range(8, 10))

        def shaped(st, like):
            if len(like.shape) == 2:
                return st[:, 0:like.shape[1]]
            k, n = like.shape[1:]
            return st[:, 0:k * n].rearrange("p (k n) -> p k n", k=k)

        def staged(n):
            return sum(16 * STAGE_GATHERS.get(m, 1) for m in range(n + 1) if buffer[m] == buffer[n])

        block = ctx.enter_context(nc.Block())

        @block.sync
        def _(sp):
            def row(ap, n):
                return ap.partition_broadcast(n)

            def gather_w(s, dt):
                for b in range(PAIR):
                    n = sp.value_load(ids[0:1, bass.ds(s.i * PAIR + (PAIR * dt + b), 1)], min_val=0, max_val=NS - 1)
                    for r in range(2):
                        sp.dma_start(wraw[C * r:C * r + C, b, :],
                                     d["wsess"][bass.ds(n, 1), :, :].rearrange("a c n -> (a c) n")).then_inc(w_in, 16)

            def gather_v(s, dt):
                for b in range(PAIR):
                    n = sp.value_load(ids[0:1, bass.ds(s.i * PAIR + (B + PAIR * dt + b), 1)], min_val=0, max_val=NC - 1)
                    sp.dma_start(vraw[C * b:C * b + C, C * b:C * b + C],
                                 d["mixw"][bass.ds(n, 1), :, :].rearrange("a c n -> (a c) n")).then_inc(v_in, 16)

            def load(s, dt, h):
                src = d["x"][bass.ds(s.i + dt, 1), :, HALF * h:HALF * h + HALF].rearrange("a p n -> (a p) n")
                if h == 0:
                    sp.dma_start(xa[:, :], src).then_inc(xa_in, 16)
                else:
                    sp.dma_start(xr[:, s.slot(dt), HALF:T], src).then_inc(x_in[s.slot(dt)], 16)

            def store(s, dt, h):
                hs = slice(HALF * h, HALF * h + HALF)
                sp.dma_start(out[bass.ds(s.i + dt, 1), :, hs].rearrange("a p n -> (a p) n"),
                             xr[:, s.slot(dt), hs]).then_inc(x_out[s.slot(dt)][h], 16)

            def step(s, gw=True, gv=True, ld=True, st=True):
                if gw:
                    sp.wait_ge(w_split, s.i + 2)
                    gather_w(s, 2)
                if gv:
                    sp.wait_ge(v_split, s.i)
                    gather_v(s, 0)
                if ld:
                    sp.wait_ge(xb_h, s.i * 2 + 3)
                    load(s, 2, 0)
                if st:
                    for h in range(2):
                        sp.wait_ge(x2_h, s.i * 2 + (h - 1))
                        store(s, -1, h)
                if ld:
                    if st:
                        sp.wait_ge(x_out[s.slot(2)][1], s.round(2) * 16)
                    load(s, 2, 1)

            def stage(n):
                src, st, done = pieces[n][0], stages[buffer[n]], stage_in[buffer[n]]
                before = last_in(buffer[n], n)
                if before is not None:
                    sp.wait_ge(stage_lo, before + 1)
                if src is not None:
                    sp.dma_start(st[:, 0:src.shape[1]], src).then_inc(done, 16)
                elif n == GATHER_A:
                    to = st[:, 0:KC * X1].rearrange("p (k n) -> p k n", k=KC)
                    for j in range(E1):
                        one = bass.ds(active[j], 1)
                        sp.dma_start(to[:, :, (R1 + 1) * j:(R1 + 1) * (j + 1)],
                                     d["a1"][one, :, :, :].rearrange("a p k r -> (a p) k r")).then_inc(done, 16)
                else:
                    for j in range(E1):
                        sp.dma_start(st[3 * R1 * j:3 * R1 * (j + 1), :], d["b1t"][bass.ds(active[j], 1), :, :]
                                     .rearrange("a r n -> (a r) n")).then_inc(done, 16)
                    sp.dma_start(st[3 * ER1:K1, :], row(d["b1"], K1 - 3 * ER1)).then_inc(done, 16)

            sp.dma_start(ids[:, :], d["ids"]).then_inc(ids_in, 16)
            sp.dma_start(per_batch[:, :, :], row(d["per_batch"], P)).then_inc(setup_in, 16)
            sp.dma_start(const[:, :], d["const"]).then_inc(setup_in, 16)
            sp.dma_start(bsess[:, :], d["bsess"]).then_inc(setup_in, 16)
            sp.dma_start(w2raw[:, :], d["w2"]).then_inc(setup_in, 16)
            for b in range(PAIR):
                sp.dma_start(b2col[C * b:C * b + C, :], d["b2"]).then_inc(setup_in, 16)
            load(at_step(0), 0, 0)
            stage(0)
            sp.wait_ge(ids_in, 16)
            gather_w(at_step(0), 0)
            stage(1)
            load(at_step(0), 0, 1)
            for n in range(2, STAGES):
                stage(n)
            sp.dma_start(b0bc[:, :], row(d["b0"], P)).then_inc(b0_in, 16)
            sp.wait_ge(v_zero, 1)
            gather_v(at_step(0), 0)
            for n in range(STAGES, L0_PIECES):
                stage(n)
                if n == 2 * STAGES:
                    sp.wait_ge(w_split, 1)
                    gather_w(at_step(0), 1)
            sp.wait_ge(stage_lo, last_in(0, L0_PIECES) + 1)
            load(at_step(0), 1, 1)
            sp.wait_ge(xb_h, 1)
            load(at_step(0), 1, 0)
            active = [sp.value_load(ids[0:1, 2 * B + j:2 * B + j + 1], min_val=0, max_val=ETOT - 1)
                      for j in range(E1)]
            for n in range(L0_PIECES, len(pieces)):
                stage(n)
                if n == L0_PIECES + 3:
                    sp.wait_ge(w_split, 2)
                    gather_w(at_step(0), 2)
                if n == L0_PIECES + 7:
                    sp.wait_ge(stage_lo, last_in(1, len(pieces)) + 1)
                    load(at_step(0), 2, 1)
                    sp.wait_ge(xb_h, 3)
                    load(at_step(0), 2, 0)
            for j in range(E1):
                sp.dma_start(picked[:, j, :], d["picks"][bass.ds(active[j], 1), :].broadcast_to([P, 2])
                             ).then_inc(pick_in, 16)
            with sp.Fori(0, (NT - 4) // RING) as q:
                for u in range(RING):
                    step(Step(q, 1 + u))
            step(at_step(NT - 3))
            step(at_step(NT - 2), gw=False, ld=False)
            step(at_step(NT - 1), gw=False, ld=False)
            step(at_step(NT), gw=False, gv=False, ld=False)
            for s in range(RING):
                for h in range(2):
                    sp.wait_ge(x_out[s][h], 16 * len(range(s, NT, RING)))

        @block.tensor
        def _(pe):
            def three(out_, left_, right_, start=True, stop=True):
                nc.tensor.matmul(out_, left_[0], right_[0], start=start, stop=False)
                nc.tensor.matmul(out_, left_[0], right_[1], start=False, stop=False)
                return nc.tensor.matmul(out_, left_[1], right_[0], start=False, stop=stop)

            def hidden(i, h):
                pe.wait_ge(xlo_h, i * 2 + (h + 1))
                if h == 0:
                    pe.wait_ge(w_split, i + 1)
                if h or not (isinstance(i, int) and i == 0):
                    pe.wait_ge(gelu_h, i * 2 + h)
                hs = slice(HALF * h, HALF * h + HALF)
                for bt in range(PAIR):
                    r = slice(C * bt, C * bt + C)
                    nc.tensor.matmul(psH[bt][:, :], wd[:, bt, :], xs[:, bt, hs], start=True, stop=False)
                    last = nc.tensor.matmul(psH[bt][:, :], wl[r, :], xs[r, bt, hs], start=False, stop=True)
                last.then_inc(hid_h, 1)

            def cond0(i, h):
                pe.wait_ge(glo_h, i * 2 + (h + 1))
                for bt in range(PAIR):
                    nc.tensor.matmul(psH[bt][:, :], w2x[bt][:, :], g[0][:, bt, :], start=True, stop=False)
                    last = nc.tensor.matmul(psH[bt][:, :], w2z[bt][:, :], g[1][:, bt, :], start=False, stop=True)
                last.then_inc(co_h, 1)

            def turn0(i, h, early=False):
                pe.wait_ge(cs_h, i * 2 + (h + 1))
                if not early:
                    pe.wait_ge(vsum_b, i * 4 - 4)
                for k in range(KH):
                    at = (KH * h + k) * P
                    last = nc.tensor.transpose(psC[h][:, k * P:(k + 1) * P], cs[:, at:at + P], ident)
                last.then_inc(turn_h, 1)

            w0k = [t[:, :].rearrange("p (k n) -> p k n", k=KC) for t in w0]
            ffns = [(c0, w0k, [(psR[0], 0, X0 + MID0), (psM[0], X0 + MID0, S0), (psM[1], X0 + MID0 + S0, S0)]),
                    (c1, w1, [(psR[1], 0, X1 + MID1), (psM[0], X1 + MID1, S1), (psM[1], X1 + MID1 + S1, S1)])]

            def ffn(layer, bank, ks):
                x, w, banks = ffns[layer]
                ps, at, n = banks[bank]
                for k in ks:
                    last = three(ps[:, 0:n], [t[:, k, :] for t in x], [t[:, k, at:at + n] for t in w],
                                 start=(k == 0), stop=(bank == 0 and k == KC - 1))
                return last

            def lora0(ps, o, n, start=False):
                return three(ps[:, 0:n], [t[:, :] for t in h0t], [t[:, o:o + n] for t in b0t], start=start)

            def lora1(ps, o, n, start=False):
                return nc.tensor.matmul(ps[:, 0:n], h1t[:, :], b1s[:, o:o + n], start=start, stop=True)

            def step(i, prep=True, l0=True, l1=True, early=False):
                if l0:
                    pe.wait_ge(c0lo_h, i * 2 + 1)
                    if l1 and not early:
                        pe.wait_ge(mid1, i - 1)
                    ffn(0, 0, range(KH))
                    pe.wait_ge(c0lo_h, i * 2 + 2)
                    ffn(0, 0, range(KH, KC)).then_inc(a0_done, 1)
                    if l1 and not early:
                        pe.wait_ge(x2_h, i * 2 - 3)
                    ffn(0, 1, range(2))
                    if prep:
                        if l1:
                            pe.wait_ge(vsum_b, i * 4)
                        hidden(i + 1, 0)
                    ffn(0, 1, range(2, KC))
                    if l1 and not early:
                        pe.wait_ge(x2_h, i * 2 - 2)
                    ffn(0, 2, range(1))
                    pe.wait_ge(hw0_done, i + 1)
                    nc.tensor.transpose(turned[0], ho0[:, :], ident).then_inc(t0_done, 1)
                    ffn(0, 2, range(1, 3))
                    if prep:
                        cond0(i + 1, 0)
                    ffn(0, 2, range(3, KC))
                    pe.wait_ge(h0lo_done, i + 1)
                    lora0(psB[0], S0, MID0, start=True)
                    lora0(psM[0], 0, S0).then_inc(m0_h, 1)
                    if prep:
                        pe.wait_ge(cs_h, i * 2 + 3)
                        hidden(i + 1, 1)
                    lora0(psM[1], S0 + MID0, S0).then_inc(m0_h, 1)
                if l1:
                    pe.wait_ge(c1lo_h, i * 2)
                    ffn(1, 0, range(KC)).then_inc(a1_done, 1)
                if l0 and prep:
                    turn0(i + 1, 0, early=not l1)
                    cond0(i + 1, 1)
                if l1:
                    if l0:
                        pe.wait_ge(x1_h, i * 2 + 1)
                    else:
                        pe.wait_ge(x2_h, i * 2 - 3)
                    ffn(1, 1, range(5))
                    pe.wait_ge(hw1_done, i)
                    nc.tensor.transpose(turned[1], f32(h1s[:, :]), ident).then_inc(t1_done, 1)
                    ffn(1, 1, range(5, KC))
                if l0 and prep:
                    turn0(i + 1, 1, early=not l1)
                if l1:
                    pe.wait_ge(h1t_done, i)
                    if l0:
                        pe.wait_ge(x1_h, i * 2 + 2)
                    else:
                        pe.wait_ge(x2_h, i * 2 - 2)
                    lora1(psB[1], S1, MID1, start=True)
                    lora1(psM[0], 0, S1).then_inc(m1_h, 1)
                    ffn(1, 2, range(KC))
                    lora1(psM[1], S1 + MID1, S1).then_inc(m1_h, 1)
                if l0:
                    pe.wait_ge(v_split, i + 1)
                    pe.wait_ge(x1lo_h, i * 2 + 2)
                    if prep:
                        pe.wait_ge(cm_h, i * 2 + 4)
                    for k in range(KC):
                        ps = psV[k // 2][:, (k % 2) * 2 * P:(k % 2 + 1) * 2 * P]
                        nc.tensor.matmul(ps, xs[:, 0, k * P:(k + 1) * P],
                                         vs[:, :, :].rearrange("p s n -> p (s n)"), start=True, stop=False)
                        last = nc.tensor.matmul(ps[:, 0:P], xs[:, 1, k * P:(k + 1) * P], vs[:, 0, :],
                                                start=False, stop=True)
                        if k % 2:
                            last.then_inc(mix_b, 1)

            pe.wait_ge(tables, 1)
            pe.wait_ge(setup_in, SETUP_IN)
            nc.tensor.matmul(psR[0][:, 0:B], bsess[:, :], onehot[:, :], start=True, stop=True).then_inc(bias_ps, 1)
            pe.wait_ge(w2_split, 1)
            for h in range(2):
                if h:
                    pe.wait_ge(cs_h, 1)
                hidden(0, h)
                cond0(0, h)
                turn0(0, h, early=True)
            pe.wait_ge(stage_lo, L0_PIECES)
            step(0, l1=False)
            pe.wait_ge(stage_lo, len(pieces))
            step(1, early=True)
            with pe.Fori(2, NT - 1) as i:
                step(i)
            step(NT - 1, prep=False)
            step(NT, prep=False, l0=False)

        @block.scalar
        def _(act):
            def hi(out_, in_):
                return nc.scalar.activation(out_, in_, ACT.Copy)

            def split_x(s, dt, h):
                hs = slice(HALF * h, HALF * h + HALF)
                if h == 0:
                    act.wait_ge(xa_in, s.i * 16 + (dt * 16 + 16))
                else:
                    act.wait_ge(x_in[s.slot(dt)], s.round(dt) * 16 + 16)
                for b in range(PAIR):
                    r = slice(C * b, C * b + C)
                    last = hi(xs[r, b, hs], xr[r, s.slot(dt), hs] if h else xa[r, :])
                last.then_inc(xhi_h, 1)

            def gelu(i, h, first=False):
                act.wait_ge(hid_h, i * 2 + (h + 1))
                if h:
                    act.wait_ge(glo_h, i * 2 + h)
                elif not first:
                    act.wait_ge(c1lo_h, i * 2 - 2)
                for bt in range(PAIR):
                    last = nc.scalar.activation(tmp[:, bt * HALF:(bt + 1) * HALF], psH[bt][:, :], ACT.Gelu,
                                                bias=hbias[:, bt:bt + 1])
                last.then_inc(gelu_h, 1)
                act.wait_ge(gelu_h, i * 2 + (h + 1))
                hi(g[0][:, :, :].rearrange("p b n -> p (b n)"), tmp[:, :]).then_inc(ghi_h, 1)

            def bias_c0(i, h):
                act.wait_ge(co_h, i * 2 + (h + 1))
                hs = slice(HALF * h, HALF * h + HALF)
                for b in range(PAIR):
                    r, q = slice(C * b, C * b + C), slice(C * (1 - b), C * (1 - b) + C)
                    last = nc.scalar.activation(cs[r, hs], psH[b][q, :], ACT.Identity, bias=b2col[q, 0:1])
                last.then_inc(part_h, 1)

            def split_c0(i, h):
                act.wait_ge(cm_h, i * 2 + (h + 1))
                hi(c0[0][:, KH * h:KH * h + KH, :].rearrange("p k n -> p (k n)"),
                   tmp[:, HALF * h:HALF * h + HALF]).then_inc(c0hi_h, 1)

            def step(s, prep=True, l0=True, l1=True, early=False, spare=None):
                i = s.i
                if l1:
                    for v in range(4):
                        act.wait_ge(mix_b, i * 4 + (v - 3))
                        hi(cs[:, 2 * P * v:2 * P * v + 2 * P].rearrange("p (k n) -> p k n", k=2),
                           psV[v][:, :].rearrange("p (k s n) -> p k s n", k=2, s=2)[:, :, 1, :]).then_inc(vlo_b, 1)
                if l1:
                    if not early:
                        act.wait_ge(m1_h, i * 2 - 2)
                    for h in range(2):
                        act.wait_ge(vsum_b, i * 4 + (2 * h - 2))
                        hi(c1[0][:, KH * h:KH * h + KH, :].rearrange("p k n -> p (k n)"),
                           tmp[:, HALF * h:HALF * h + HALF]).then_inc(c1hi_h, 1)
                if prep:
                    split_x(s, 1, 0)
                if spare:
                    for n in SPARE[0]:
                        spare(n)
                if l0:
                    act.wait_ge(gap_done, i + 1)
                    nc.scalar.activation(egap[:, :], gap[:, :], ACT.Exp).then_inc(egap_done, 1)
                if prep:
                    nc.scalar.activation(ahead[:, :], const[:, C_P:C_P + 1], ACT.Gelu)
                if prep:
                    gelu(i + 1, 0, first=not l1)
                    split_x(s, 1, 1)
                if l0:
                    act.wait_ge(t0_done, i + 1)
                    hi(h0t[0][:, :], turned[0]).then_inc(h0hi_done, 1)
                if prep:
                    bias_c0(i + 1, 0)
                if spare:
                    for n in SPARE[1]:
                        spare(n)
                if prep:
                    gelu(i + 1, 1)
                    nc.scalar.activation(ahead[:, :], const[:, C_CH:C_CH + 1], ACT.Exp)
                if l0:
                    for h in range(2):
                        hs = slice(HALF * h, HALF * h + HALF)
                        act.wait_ge(x1_h, i * 2 + (h + 1))
                        hi(xs[:, 0, hs], xr[:, s.slot(0), hs]).then_inc(x1hi_h, 1)
                if spare:
                    for n in SPARE[2]:
                        spare(n)
                if l1:
                    act.wait_ge(nmax_done, i)
                    nc.scalar.activation(ez[:, :], z1[:, :], ACT.Exp, bias=nmax[:, 0:1],
                                         accum_out=zsum[:, :]).then_inc(ez_done, 1)
                if prep:
                    bias_c0(i + 1, 1)
                if l1:
                    act.wait_ge(t1_done, i)
                    hi(h1t[:, :], turned[1]).then_inc(h1t_done, 1)
                if prep:
                    act.wait_ge(m0_h, i * 2 + 2)
                    for h in range(2):
                        split_c0(i + 1, h)
                if spare:
                    for n in SPARE[3]:
                        spare(n)

            act.wait_ge(setup_in, SETUP_IN)
            act.wait_ge(w2_zero, 1)
            for b in range(PAIR):
                hi(w2z[b][:, C * b:C * b + C], w2raw[:, :])
                last = hi(w2x[b][:, C * b:C * b + C], w2raw[:, :])
            last.then_inc(w2_hi, 1)

            def piece(n):
                _src, hi_, _lo = pieces[n]
                st = stages[buffer[n]]
                act.wait_ge(stage_in[buffer[n]], staged(n))
                if n == GATHER_B:
                    hi(b1s[:, :], st[0:K1, :]).then_inc(stage_hi, 1)
                else:
                    hi(hi_, shaped(st, hi_)).then_inc(stage_hi, 1)

            nc.scalar.activation(ahead[:, :], const[:, C_P:C_P + 1], ACT.Gelu)
            between = {0: lambda: split_x(at_step(0), 0, 0), 1: lambda: split_x(at_step(0), 0, 1),
                       3: lambda: gelu(0, 0, first=True), 6: lambda: bias_c0(0, 0),
                       8: lambda: gelu(0, 1), 10: lambda: bias_c0(0, 1)}
            for n in range(L0_PIECES):
                piece(n)
                if n in between:
                    between[n]()
            for h in range(2):
                split_c0(0, h)
            step(at_step(0), l1=False, spare=lambda n: piece(L0_PIECES + n))
            act.wait_ge(tables, 4)
            nc.scalar.activation(prior, prior, ACT.Ln).then_inc(logits_in, 1)
            step(at_step(1), early=True)
            step(at_step(2))
            step(at_step(3))
            with act.Fori(1, NT // RING - 1) as q:
                for u in range(RING):
                    step(Step(q, 1 + u))
            for i in range(RING * (NT // RING - 1) + 1, NT - 1):
                step(at_step(i))
            step(at_step(NT - 1), prep=False)
            step(at_step(NT), prep=False, l0=False)

        @block.vector
        def _(dve):
            tt, ts, stt = nc.vector.tensor_tensor, nc.vector.tensor_scalar, nc.vector.scalar_tensor_tensor

            def lo(out_, in_, hi_):
                return tt(out_, in_, f32(hi_), ALU.subtract)

            def split_w(i, first=False):
                dve.wait_ge(w_in, i * (32 * PAIR) + 32 * PAIR)
                if not first:
                    dve.wait_ge(hid_h, i * 2)
                ts(hbias[:, :], sess_bias[:, bass.ds(i * PAIR, PAIR)], 1.0, None, ALU.mult)
                for b in range(PAIR):
                    last = ts(wd[:, b, :], wraw[:, b, :], cmask[:, bass.ds(i * PAIR + b, 1)], None, ALU.mult)
                last.then_inc(ws_hi, 1)
                dve.wait_ge(ws_hi, i + 1)
                for b in range(PAIR):
                    r = slice(C * b, C * b + C)
                    last = stt(wl[r, :], wraw[r, b, :], cmask[r, bass.ds(i * PAIR + b, 1)], f32(wd[r, b, :]),
                               ALU.mult, ALU.subtract)
                last.then_inc(w_split, 1)

            def split_v(i):
                dve.wait_ge(v_in, i * (16 * PAIR) + 16 * PAIR)
                nc.vector.tensor_copy(vs[:, 0, :], vraw[:, :]).then_inc(vs_hi, 1)
                dve.wait_ge(vs_hi, i + 1)
                lo(vs[:, 1, :], vraw[:, :], vs[:, 0, :]).then_inc(v_split, 1)

            def split_x(s, dt, h):
                hs = slice(HALF * h, HALF * h + HALF)
                dve.wait_ge(xhi_h, s.i * 2 + (2 * dt + h + 1))
                for b in range(PAIR):
                    r, q = slice(C * b, C * b + C), slice(C * (1 - b), C * (1 - b) + C)
                    last = lo(xs[q, b, hs], xr[r, s.slot(dt), hs] if h else xa[r, :], xs[r, b, hs])
                last.then_inc(xlo_h, 1)

            def split_g(i, h):
                dve.wait_ge(ghi_h, i * 2 + (h + 1))
                lo(g[1][:, :, :].rearrange("p b n -> p (b n)"), tmp[:, :],
                   g[0][:, :, :].rearrange("p b n -> p (b n)")).then_inc(glo_h, 1)

            def sum_c0(i, h):
                dve.wait_ge(part_h, i * 2 + (h + 1))
                hs = slice(HALF * h, HALF * h + HALF)
                for b in range(PAIR):
                    r = slice(C * b, C * b + C)
                    last = tt(cs[r, hs], psH[b][r, :], cs[r, hs], ALU.add)
                last.then_inc(cs_h, 1)

            def mask_c0(i, h):
                dve.wait_ge(turn_h, i * 2 + (h + 1))
                dve.wait_ge(glo_h, i * 2 + 2)
                m = tmask[:, bass.ds(i, 1), h * (HALF // C):(h + 1) * (HALF // C)].rearrange("p a m -> p (a m)")
                tt(tmp[:, HALF * h:HALF * h + HALF].rearrange("p (m s) -> p m s", s=C),
                   psC[h][:, :].rearrange("p (m s) -> p m s", s=C),
                   m.unsqueeze(2).to_broadcast([P, HALF // C, C]), ALU.mult).then_inc(cm_h, 1)

            def split_c0(i, h):
                dve.wait_ge(c0hi_h, i * 2 + (h + 1))
                t = slice(KH * h, KH * h + KH)
                lo(c0[1][:, t, :].rearrange("p k n -> p (k n)"), tmp[:, HALF * h:HALF * h + HALF],
                   c0[0][:, t, :].rearrange("p k n -> p (k n)")).then_inc(c0lo_h, 1)

            ROUTE0, ROUTE1 = 13, 5

            def route_0(i):
                done = [0]

                def link(ins, sync=True):
                    done[0] += 1
                    ins.then_inc(route0, 1)
                    if sync:
                        dve.wait_ge(route0, i * ROUTE0 + done[0])

                dve.wait_ge(a0_done, i + 1)
                link(nc.vector.tensor_copy(lg[:, :], psR[0][:, ER0:X0]))
                nc.vector.tensor_copy(ho0[:, :], psR[0][:, 0:ER0])
                link(nc.vector.max(top[:, :], lg[:, :]))
                tt(gap[:, :], top[:, 1:2], top[:, 0:1], ALU.subtract).then_inc(gap_done, 1)
                link(stt(pick[0][:, :], lg[:, :], top[:, 0:1], rank, ALU.is_equal, ALU.mult))
                link(nc.vector.tensor_reduce(first[0][:, :], pick[0][:, :], AX_X, ALU.max))
                link(stt(left[:, :], rank, first[0][:, 0:1], rank, ALU.not_equal, ALU.mult))
                link(stt(pick[1][:, :], lg[:, :], top[:, 1:2], left[:, :], ALU.is_equal, ALU.mult))
                link(nc.vector.tensor_reduce(first[1][:, :], pick[1][:, :], AX_X, ALU.max), sync=False)
                dve.wait_ge(egap_done, i + 1)
                link(ts(esum[:, :], egap[:, :], 1.0, 1.0 / SCALING, ALU.add, ALU.mult))
                link(nc.vector.reciprocal(wtop[0][:, :], esum[:, :]))
                link(ts(wtop[1][:, :], egap[:, :], wtop[0][:, 0:1], None, ALU.mult), sync=False)
                link(ts(wsel[0][:, :], rank, first[0][:, 0:1], wtop[0][:, 0:1], ALU.is_equal, ALU.mult))
                link(ts(wsel[1][:, :], rank, first[1][:, 0:1], wtop[1][:, 0:1], ALU.is_equal, ALU.mult))
                link(tt(wsum[:, :], wsel[0][:, :], wsel[1][:, :], ALU.add))
                assert done[0] == ROUTE0
                tt(ho0[:, :].rearrange("p (e r) -> p e r", e=E0),
                   ho0[:, :].rearrange("p (e r) -> p e r", e=E0),
                   wsum[:, :].unsqueeze(2).to_broadcast([P, E0, R0]), ALU.mult).then_inc(hw0_done, 1)

            out1 = psR[1][:, 0:X1].rearrange("p (e r) -> p e r", e=E1)

            def link_1(i, n, ins):
                ins.then_inc(route1, 1)
                dve.wait_ge(route1, i * ROUTE1 + n)

            def logits_1(i):
                dve.wait_ge(a1_done, i + 1)
                link_1(i, 1, tt(z1[:, :], out1[:, :, R1:R1 + 1].rearrange("p e r -> p (e r)"),
                                logit_bias[:, :], ALU.add))
                nc.vector.tensor_reduce(nmax[:, :], z1[:, :], AX_X, ALU.max, negate=True).then_inc(nmax_done, 1)

            def route_1(i):
                dve.wait_ge(ez_done, i + 1)
                link_1(i, 2, nc.vector.reciprocal(zinv[:, :], zsum[:, :]))
                link_1(i, 3, ts(alpha[:, :], ez[:, :], zinv[:, 0:1], SCALING, ALU.mult, ALU.mult))
                link_1(i, 4, tt(hw1, out1[:, :, 0:R1], alpha[:, :].unsqueeze(2).to_broadcast([P, E1, R1]), ALU.mult))
                stack = h1s[:, 0:3 * ER1].rearrange("p (e s r) -> p s e r", s=3, e=E1)
                link_1(i, ROUTE1, nc.vector.tensor_copy(stack[:, 0], hw1))
                nc.vector.tensor_copy(stack[:, 2], hw1)
                lo(stack[:, 1], hw1, stack[:, 0]).then_inc(hw1_done, 1)

            def split_c1(i, h):
                t = slice(KH * h, KH * h + KH)
                dve.wait_ge(c1hi_h, i * 2 + (h + 1))
                lo(c1[1][:, t, :].rearrange("p k n -> p (k n)"), tmp[:, HALF * h:HALF * h + HALF],
                   c1[0][:, t, :].rearrange("p k n -> p (k n)")).then_inc(c1lo_h, 1)

            def step(s, prep=True, l0=True, l1=True, more=True, spare=None):
                i = s.i

                def add(slot, out_, ps, at=0):
                    x = xr[:, s.slot(slot), out_]
                    return tt(x, x, ps[:, at:at + out_.stop - out_.start], ALU.add)

                def add_x1(h):
                    dve.wait_ge(m0_h, i * 2 + (h + 1))
                    if h == 0:
                        dve.wait_ge(xb_h, i * 2 + 2)
                        add(0, slice(S0, S0 + MID0), psB[0]).then_inc(mid0, 1)
                        dve.wait_ge(mid0, i + 1)
                        add(0, slice(S0, S0 + MID0), psR[0], X0)
                        add(0, slice(0, S0), psM[0]).then_inc(x1_h, 1)
                    else:
                        add(0, slice(S0 + MID0, O), psM[1]).then_inc(x1_h, 1)

                def add_x2(h):
                    dve.wait_ge(m1_h, i * 2 + (h - 1))
                    if h == 0:
                        add(-1, slice(S1, S1 + MID1), psB[1]).then_inc(mid1, 1)
                        dve.wait_ge(mid1, i)
                        add(-1, slice(S1, S1 + MID1), psR[1], X1)
                        add(-1, slice(0, S1), psM[0]).then_inc(x2_h, 1)
                    else:
                        add(-1, slice(S1 + MID1, O), psM[1]).then_inc(x2_h, 1)

                if l1:
                    if l0:
                        dve.wait_ge(c0lo_h, i * 2 + 2)
                    else:
                        dve.wait_ge(c1lo_h, i * 2 - 2)
                    for v in range(4):
                        dve.wait_ge(vlo_b, i * 4 + (v - 3))
                        tt(tmp[:, 2 * P * v:2 * P * v + 2 * P].rearrange("p (k n) -> p k n", k=2),
                           psV[v][:, :].rearrange("p (k s n) -> p k s n", k=2, s=2)[:, :, 0, :],
                           cs[:, 2 * P * v:2 * P * v + 2 * P].rearrange("p (k n) -> p k n", k=2),
                           ALU.add).then_inc(vsum_b, 1)
                if l1:
                    for h in range(2):
                        split_c1(i - 1, h)
                if prep:
                    split_x(s, 1, 0)
                if spare:
                    for n in SPARE[0]:
                        spare(n)
                if l0:
                    route_0(i)
                if prep:
                    split_g(i + 1, 0)
                if l0:
                    dve.wait_ge(h0hi_done, i + 1)
                    lo(h0t[1][:, :], turned[0], h0t[0][:, :]).then_inc(h0lo_done, 1)
                if prep:
                    split_x(s, 1, 1)
                    sum_c0(i + 1, 0)
                if spare:
                    for n in SPARE[1]:
                        spare(n)
                if l0:
                    for h in range(2):
                        add_x1(h)
                if prep:
                    split_g(i + 1, 1)
                if l1:
                    logits_1(i - 1)
                if l0:
                    for h in range(2):
                        hs = slice(HALF * h, HALF * h + HALF)
                        dve.wait_ge(x1hi_h, i * 2 + (h + 1))
                        lo(xs[:, 1, hs], xr[:, s.slot(0), hs], xs[:, 0, hs]).then_inc(x1lo_h, 1)
                if spare:
                    for n in SPARE[2]:
                        spare(n)
                if l1:
                    route_1(i - 1)
                if prep:
                    sum_c0(i + 1, 1)
                    mask_c0(i + 1, 0)
                if l0:
                    split_v(i)
                if prep:
                    split_c0(i + 1, 0)
                if l1:
                    add_x2(0)
                if prep:
                    mask_c0(i + 1, 1)
                    if more:
                        split_w(i + 2)
                    split_c0(i + 1, 1)
                if spare:
                    for n in SPARE[3]:
                        spare(n)
                if l1:
                    add_x2(1)

            nc.vector.memset(vraw[:, :], 0.0).then_inc(v_zero, 1)
            for b in range(PAIR):
                last = nc.vector.memset(f32(w2z[b][:, :]), 0.0)
            last.then_inc(w2_zero, 1)
            dve.wait_ge(setup_in, SETUP_IN)
            ts(onehot[:, :], sess8, const[0:NS, C_P:C_P + 1], None, ALU.is_equal).then_inc(tables, 1)
            ts(cmask[:, :], lens, const[:, C_CH:C_CH + 1], None, ALU.is_gt).then_inc(tables, 1)
            def piece(n):
                _src, _hi, lo_ = pieces[n]
                dve.wait_ge(stage_hi, n + 1)
                st = stages[buffer[n]]
                if n == GATHER_B:
                    stt(b1s[:, :], f32(b1s[:, :]), const[0:K1, C_NLO:C_NLO + 1], st[0:K1, :],
                        ALU.mult, ALU.add).then_inc(stage_lo, 1)
                else:
                    lo(lo_, shaped(st, lo_), _hi).then_inc(stage_lo, 1)

            piece(0)
            dve.wait_ge(bias_ps, 1)
            nc.vector.tensor_copy(sess_bias[:, :], psR[0][:, 0:B]).then_inc(tables, 1)
            dve.wait_ge(tables, 3)
            split_w(0, first=True)
            dve.wait_ge(w2_hi, 1)
            for b in range(PAIR):
                last = lo(w2x[b][:, C * (1 - b):C * (1 - b) + C], w2raw[:, :], w2x[b][:, C * b:C * b + C])
            last.then_inc(w2_split, 1)

            between = {1: lambda: split_x(at_step(0), 0, 1), 3: lambda: split_g(0, 0), 6: lambda: sum_c0(0, 0),
                       8: lambda: split_g(0, 1), 10: lambda: sum_c0(0, 1)}
            split_x(at_step(0), 0, 0)
            for n in range(1, L0_PIECES):
                piece(n)
                if n in between:
                    between[n]()
                if n == 7:
                    m = tmask[:, :, :].rearrange("p n (k b) -> p n k b", b=PAIR)
                    for k in range(KC):
                        last = ts(m[:, :, k, :], seqs.rearrange("p (n b) -> p n b", b=PAIR),
                                  const[:, C_T + k:C_T + k + 1], None, ALU.is_gt)
                    last.then_inc(tmask_done, 1)
            dve.wait_ge(tmask_done, 1)
            for h in range(2):
                mask_c0(0, h)
                split_c0(0, h)
            split_w(1)
            nc.vector.memset(f32(h1s[:, 3 * ER1:K1]), 1.0)
            step(at_step(0), l1=False, spare=lambda n: piece(L0_PIECES + n))
            dve.wait_ge(pick_in, 16 * E1)
            ts(prior, prior, EPS, None, ALU.add).then_inc(tables, 1)
            dve.wait_ge(logits_in, 1)
            tt(logit_bias[:, :], prior, rbias, ALU.add).then_inc(logit_bias_done, 1)
            dve.wait_ge(logit_bias_done, 1)
            with dve.Fori(0, NT // RING - 1) as q:
                for u in range(RING):
                    step(Step(q, 1 + u))
            for i in range(RING * (NT // RING - 1) + 1, NT - 1):
                step(at_step(i), more=i + 2 < NT)
            step(at_step(NT - 1), prep=False)
            step(at_step(NT), prep=False, l0=False)

        @block.gpsimd
        def _(pool):
            def bias_x(s, dt, h, free=True):
                hs = slice(HALF * h, HALF * h + HALF)
                to = xr[:, s.slot(dt), hs]
                pool.wait_ge(xlo_h, s.i * 2 + (2 * dt + h + 1))
                if h == 0 and not free:
                    pool.wait_ge(x_out[s.slot(dt)][0], s.round(dt) * 16)
                nc.gpsimd.tensor_tensor(to, to if h else xa[:, :], b0bc[:, hs], ALU.add).then_inc(xb_h, 1)

            pool.wait_ge(b0_in, 16)
            for i in range(RING):
                for h in range(2):
                    bias_x(at_step(i), 0, h)
            with pool.Fori(1, NT // RING) as q:
                for u in range(RING):
                    for h in range(2):
                        bias_x(Step(q, u), 0, h, free=False)
            for i in range(NT // RING * RING, NT):
                for h in range(2):
                    bias_x(at_step(i), 0, h, free=False)


def kernel(**inputs):
    import concourse.bacc as bacc
    from concourse.bass_utils import run_bass_kernel_spmd

    a = {k: np.ascontiguousarray(v) for k, v in inputs.items()}
    sess, seqs, cond, lens = a["itok_B_0_7"], a["itok_B_2182_4065"], a["itok_B_0_15"], a["_lenS"]
    laid = {
        "x": a["x"].reshape(NT, P, T),
        "ids": np.concatenate([sess, cond, a["L1_ffn_active"]])[None, :],
        "per_batch": np.stack([sess, lens, seqs]),
        "const": constants(),
        "wsess": a["L0_cond_W_sess"],
        "bsess": a["L0_cond_b_sess"],
        "w2": a["L0_cond_W2"],
        "b2": a["L0_cond_b2"][:, None],
        "w0": np.concatenate([a["L0_ffn_A"].reshape(ER0, T), a["L0_ffn_W_router"],
                              a["L0_ffn_W_base"][S0:S0 + MID0], a["L0_ffn_W_base"][:S0],
                              a["L0_ffn_W_base"][S0 + MID0:]]).T
              .reshape(KC, P, N0).transpose(1, 0, 2).reshape(P, KC * N0),
        "b0": a["L0_ffn_b_base"],
        "b0t": a["L0_ffn_B"].transpose(0, 2, 1).reshape(ER0, O),
        "mixw": a["L1_cond_weights"],
        "w1": np.concatenate([a["L1_ffn_W_base"][S1:S1 + MID1], a["L1_ffn_W_base"][:S1],
                              a["L1_ffn_W_base"][S1 + MID1:]]).T,
        "b1": a["L1_ffn_b_base"],
        "a1": np.concatenate([a["L1_ffn_lora_A"].reshape(ETOT, R1, KC, P),
                              a["L1_ffn_router_W"].reshape(ETOT, 1, KC, P)], axis=1).transpose(0, 3, 2, 1),
        "b1t": np.tile(a["L1_ffn_lora_B"].transpose(0, 2, 1), (1, 3, 1)),
        "picks": np.stack([a["L1_ffn_domain_prior"], a["L1_ffn_router_b"]], axis=1),
    }
    nc = bacc.Bacc("TRN2", target_bir_lowering=False, num_devices=1, dynamic_dma_scratch_size=1024)
    arrays, d = {}, {}
    for name, v in laid.items():
        v = np.ascontiguousarray(v)
        arrays[f"in_{name}"] = v
        d[name] = nc.dram_tensor(f"in_{name}", v.shape, mybir.dt.from_np(v.dtype), kind="ExternalInput").ap()
    out = nc.dram_tensor("out", (NT, P, T), F32, kind="ExternalOutput").ap()
    build(nc, d, out)
    r = run_bass_kernel_spmd(nc, [arrays], core_ids=[0])
    return r.results[0]["out"].reshape(B, C, T)
```
